# Optimizing a Trainium2 kernel written in Bass

```python
import numpy as np
import jax
import jax.numpy as jnp

def _softmax(x, axis=-1):
    return jax.nn.softmax(x, axis=axis)

def _gelu(x):
    return jax.nn.gelu(x, approximate=True)

def _silu(x):
    return jax.nn.silu(x)

def _sigmoid(x):
    return jax.nn.sigmoid(x)

def _layernorm(x, axis=-1, eps=1e-05):
    m = jnp.mean(x, axis=axis, keepdims=True)
    v = jnp.var(x, axis=axis, keepdims=True)
    return (x - m) / jnp.sqrt(v + eps)

def _scatter_add(tgt, idx, src, axis=0):
    return tgt.at[idx].add(src)

def _segment_sum(src, seg, n):
    return jax.ops.segment_sum(src, seg, n)
kernel_name = 'mk_flamingo_gated_d1_seqx_r4_7e499d'

def setup_inputs(seed: int=0):
    np.random.seed(seed)
    _w = jnp.asarray

    def _rec_inputs():
        import jax
        import jax.numpy as jnp
        _rk = jax.random.key(seed)
        x = 7.22e-05 + 1 * jax.random.normal(jax.random.fold_in(_rk, 1), (16, 128, 512), jnp.float32)
        _lenS = 128 - jax.random.randint(jax.random.fold_in(_rk, 7), (16,), 0, max(1, 128 // 4) + 1, jnp.int32)
        _lenS2 = 128 - jax.random.randint(jax.random.fold_in(_rk, 8), (16,), 0, max(1, 128 // 4) + 1, jnp.int32)
        _ctx_2048P = jax.random.normal(jax.random.fold_in(_rk, 11), (16, 16, 512), jnp.float32)
        _ctx_2048c = jax.random.dirichlet(jax.random.fold_in(_rk, 511), 0.3 * jnp.ones((16,), jnp.float32), (16, 128))
        _ctx_2048t = jnp.einsum('bsk,bkd->bsd', _ctx_2048c, _ctx_2048P)
        _ctx_2048t = _ctx_2048t * jax.lax.rsqrt(jnp.mean(jnp.square(_ctx_2048t)) + 1e-12) * 0.953939
        ctx_2048 = 4.13588e-05 + 0.999923 * (_ctx_2048t + 0.3 * jax.random.normal(jax.random.fold_in(_rk, 611), (16, 128, 512), jnp.float32))
        _g = jax.random.normal(jax.random.fold_in(_rk, 9001), (2, 1), jnp.float32)
        _g = jnp.sign(_g) * jnp.maximum(jnp.abs(_g), 1.0) + (_g == 0) * 1.0
        g_xattn = _g[0]
        g_ffn = _g[1]
        return (x, ctx_2048, g_xattn, g_ffn)
    x, ctx_2048, g_xattn, g_ffn = _rec_inputs()

    def _L0_xattn_setup():
        import jax, jax.numpy as jnp
        import numpy as np
        N_HEAD = 8
        key = jax.random.key(seed)
        k1, k2, k3 = jax.random.split(key, 3)
        B, D, L = (4, 256, 512)
        q = jax.random.normal(k1, (B, D, L), dtype=jnp.float32)
        k = jax.random.normal(k2, (B, D, L), dtype=jnp.float32)
        v = jax.random.normal(k3, (B, D, L), dtype=jnp.float32)
        gamma = jnp.ones((), dtype=jnp.float32)
        return {'q': q, 'k': k, 'v': v, 'gamma': gamma}
    _L0_xattn_all = _L0_xattn_setup()
    _L0_xattn_in = {k: v for k, v in _L0_xattn_all.items() if k in ('gamma',)}
    del _L0_xattn_all

    def _L0_ffn_setup():
        import jax, jax.numpy as jnp
        import numpy as np
        COST_LAMBDA = 1e-07
        HID = [256, 512, 768, 1024, 256, 512, 768, 1024]
        TOP_K = 2

        def _gelu(v):
            return jax.nn.gelu(v, approximate=False)

        def _forward(x, down_w, down_b, up_w, up_b, router_w, router_b, shared_w1, shared_b1, shared_w2, shared_b2, core_w, core_b, expert_params):
            E = len(expert_params)
            h = x @ down_w + down_b
            cost = jnp.array([w1.shape[0] * w1.shape[1] + w2.shape[0] * w2.shape[1] for w1, _, w2, _ in expert_params], jnp.float32)
            logits = x @ router_w + router_b - COST_LAMBDA * cost
            probs = jax.nn.softmax(logits, axis=-1)
            topv, topi = jax.lax.top_k(probs, TOP_K)
            gate = jax.nn.softmax(topv, axis=-1)
            out = jnp.zeros_like(h)
            for k in range(TOP_K):
                mask = jax.nn.one_hot(topi[..., k], E, dtype=h.dtype)
                acc = jnp.zeros_like(h)
                for e, (w1, b1, w2, b2) in enumerate(expert_params):
                    hm = h * mask[..., e:e + 1]
                    acc = acc + (_gelu(_gelu(hm) @ w1 + b1) @ w2 + b2)
                out = out + acc * gate[..., k:k + 1]
            out = out + 0.1 * (_gelu(_gelu(h) @ shared_w1 + shared_b1) @ shared_w2 + shared_b2)
            out = out @ up_w + up_b
            out = out + (_gelu(x) @ core_w + core_b)
            return out
        key = jax.random.key(seed)
        ks = iter(jax.random.split(key, 80))

        def W(shape):
            return jax.random.normal(next(ks), shape, jnp.float32) * 0.02
        B, T, D, L = (4, 512, 512, 256)
        inp = {'x': jax.random.normal(next(ks), (B, T, D), jnp.float32)}
        inp['down_w'] = W((D, L))
        inp['down_b'] = jnp.zeros((L,), jnp.float32)
        inp['up_w'] = W((L, D))
        inp['up_b'] = jnp.zeros((D,), jnp.float32)
        inp['router_w'] = W((D, len(HID)))
        inp['router_b'] = jnp.zeros((len(HID),), jnp.float32)
        inp['shared_w1'] = W((L, L))
        inp['shared_b1'] = jnp.zeros((L,), jnp.float32)
        inp['shared_w2'] = W((L, L))
        inp['shared_b2'] = jnp.zeros((L,), jnp.float32)
        inp['core_w'] = W((D, D))
        inp['core_b'] = jnp.zeros((D,), jnp.float32)
        for e, h in enumerate(HID):
            inp[f'e{e}_w1'] = W((L, h))
            inp[f'e{e}_b1'] = jnp.zeros((h,), jnp.float32)
            inp[f'e{e}_w2'] = W((h, L))
            inp[f'e{e}_b2'] = jnp.zeros((L,), jnp.float32)
        return inp
    _L0_ffn_all = _L0_ffn_setup()
    _L0_ffn_in = {k: v for k, v in _L0_ffn_all.items() if k in ('down_w', 'down_b', 'up_w', 'up_b', 'router_w', 'router_b', 'shared_w1', 'shared_b1', 'shared_w2', 'shared_b2', 'core_w', 'core_b', 'e0_w1', 'e0_b1', 'e0_w2', 'e0_b2', 'e1_w1', 'e1_b1', 'e1_w2', 'e1_b2', 'e2_w1', 'e2_b1', 'e2_w2', 'e2_b2', 'e3_w1', 'e3_b1', 'e3_w2', 'e3_b2', 'e4_w1', 'e4_b1', 'e4_w2', 'e4_b2', 'e5_w1', 'e5_b1', 'e5_w2', 'e5_b2', 'e6_w1', 'e6_b1', 'e6_w2', 'e6_b2', 'e7_w1', 'e7_b1', 'e7_w2', 'e7_b2')}
    del _L0_ffn_all
    return {'x': x, 'ctx_2048': ctx_2048, 'g_xattn': g_xattn, 'g_ffn': g_ffn, 'L0_xattn_gamma': _L0_xattn_in['gamma'], 'L0_ffn_down_w': _L0_ffn_in['down_w'], 'L0_ffn_down_b': _L0_ffn_in['down_b'], 'L0_ffn_up_w': _L0_ffn_in['up_w'], 'L0_ffn_up_b': _L0_ffn_in['up_b'], 'L0_ffn_router_w': _L0_ffn_in['router_w'], 'L0_ffn_router_b': _L0_ffn_in['router_b'], 'L0_ffn_shared_w1': _L0_ffn_in['shared_w1'], 'L0_ffn_shared_b1': _L0_ffn_in['shared_b1'], 'L0_ffn_shared_w2': _L0_ffn_in['shared_w2'], 'L0_ffn_shared_b2': _L0_ffn_in['shared_b2'], 'L0_ffn_core_w': _L0_ffn_in['core_w'], 'L0_ffn_core_b': _L0_ffn_in['core_b'], 'L0_ffn_e0_w1': _L0_ffn_in['e0_w1'], 'L0_ffn_e0_b1': _L0_ffn_in['e0_b1'], 'L0_ffn_e0_w2': _L0_ffn_in['e0_w2'], 'L0_ffn_e0_b2': _L0_ffn_in['e0_b2'], 'L0_ffn_e1_w1': _L0_ffn_in['e1_w1'], 'L0_ffn_e1_b1': _L0_ffn_in['e1_b1'], 'L0_ffn_e1_w2': _L0_ffn_in['e1_w2'], 'L0_ffn_e1_b2': _L0_ffn_in['e1_b2'], 'L0_ffn_e2_w1': _L0_ffn_in['e2_w1'], 'L0_ffn_e2_b1': _L0_ffn_in['e2_b1'], 'L0_ffn_e2_w2': _L0_ffn_in['e2_w2'], 'L0_ffn_e2_b2': _L0_ffn_in['e2_b2'], 'L0_ffn_e3_w1': _L0_ffn_in['e3_w1'], 'L0_ffn_e3_b1': _L0_ffn_in['e3_b1'], 'L0_ffn_e3_w2': _L0_ffn_in['e3_w2'], 'L0_ffn_e3_b2': _L0_ffn_in['e3_b2'], 'L0_ffn_e4_w1': _L0_ffn_in['e4_w1'], 'L0_ffn_e4_b1': _L0_ffn_in['e4_b1'], 'L0_ffn_e4_w2': _L0_ffn_in['e4_w2'], 'L0_ffn_e4_b2': _L0_ffn_in['e4_b2'], 'L0_ffn_e5_w1': _L0_ffn_in['e5_w1'], 'L0_ffn_e5_b1': _L0_ffn_in['e5_b1'], 'L0_ffn_e5_w2': _L0_ffn_in['e5_w2'], 'L0_ffn_e5_b2': _L0_ffn_in['e5_b2'], 'L0_ffn_e6_w1': _L0_ffn_in['e6_w1'], 'L0_ffn_e6_b1': _L0_ffn_in['e6_b1'], 'L0_ffn_e6_w2': _L0_ffn_in['e6_w2'], 'L0_ffn_e6_b2': _L0_ffn_in['e6_b2'], 'L0_ffn_e7_w1': _L0_ffn_in['e7_w1'], 'L0_ffn_e7_b1': _L0_ffn_in['e7_b1'], 'L0_ffn_e7_w2': _L0_ffn_in['e7_w2'], 'L0_ffn_e7_b2': _L0_ffn_in['e7_b2']}

def reference(x, ctx_2048, g_xattn, g_ffn, L0_xattn_gamma, L0_ffn_down_w, L0_ffn_down_b, L0_ffn_up_w, L0_ffn_up_b, L0_ffn_router_w, L0_ffn_router_b, L0_ffn_shared_w1, L0_ffn_shared_b1, L0_ffn_shared_w2, L0_ffn_shared_b2, L0_ffn_core_w, L0_ffn_core_b, L0_ffn_e0_w1, L0_ffn_e0_b1, L0_ffn_e0_w2, L0_ffn_e0_b2, L0_ffn_e1_w1, L0_ffn_e1_b1, L0_ffn_e1_w2, L0_ffn_e1_b2, L0_ffn_e2_w1, L0_ffn_e2_b1, L0_ffn_e2_w2, L0_ffn_e2_b2, L0_ffn_e3_w1, L0_ffn_e3_b1, L0_ffn_e3_w2, L0_ffn_e3_b2, L0_ffn_e4_w1, L0_ffn_e4_b1, L0_ffn_e4_w2, L0_ffn_e4_b2, L0_ffn_e5_w1, L0_ffn_e5_b1, L0_ffn_e5_w2, L0_ffn_e5_b2, L0_ffn_e6_w1, L0_ffn_e6_b1, L0_ffn_e6_w2, L0_ffn_e6_b2, L0_ffn_e7_w1, L0_ffn_e7_b1, L0_ffn_e7_w2, L0_ffn_e7_b2):
    import jax
    import jax.numpy as jnp

    def _L0_xattn_ref(q, k, v, gamma):
        import jax, jax.numpy as jnp
        import numpy as np
        N_HEAD = 8
        B, Dq, Lq = q.shape
        Dv, Lk = (v.shape[-2], v.shape[-1])
        h = N_HEAD
        dq = Dq // h
        dv = Dv // h
        qh = q.reshape(B, h, dq, Lq)
        kh = k.reshape(B, h, dq, Lk)
        vh = v.reshape(B, h, dv, Lk)
        scale = 1.0 / jnp.sqrt(jnp.asarray(dq, dtype=q.dtype))
        qk = jnp.einsum('bhdq,bhdl->bhql', qh, kh) * scale
        sm = jax.nn.softmax(qk, axis=-1)
        ret = jnp.einsum('bhql,bhdl->bhdq', sm, vh)
        ret = ret.reshape(B, Dv, Lq)
        return gamma * ret

    def _L0_ffn_ref(x, down_w, down_b, up_w, up_b, router_w, router_b, shared_w1, shared_b1, shared_w2, shared_b2, core_w, core_b, e0_w1, e0_b1, e0_w2, e0_b2, e1_w1, e1_b1, e1_w2, e1_b2, e2_w1, e2_b1, e2_w2, e2_b2, e3_w1, e3_b1, e3_w2, e3_b2, e4_w1, e4_b1, e4_w2, e4_b2, e5_w1, e5_b1, e5_w2, e5_b2, e6_w1, e6_b1, e6_w2, e6_b2, e7_w1, e7_b1, e7_w2, e7_b2):
        import jax, jax.numpy as jnp
        import numpy as np
        COST_LAMBDA = 1e-07
        HID = [256, 512, 768, 1024, 256, 512, 768, 1024]
        TOP_K = 2

        def _gelu(v):
            return jax.nn.gelu(v, approximate=False)

        def _forward(x, down_w, down_b, up_w, up_b, router_w, router_b, shared_w1, shared_b1, shared_w2, shared_b2, core_w, core_b, expert_params):
            E = len(expert_params)
            h = x @ down_w + down_b
            cost = jnp.array([w1.shape[0] * w1.shape[1] + w2.shape[0] * w2.shape[1] for w1, _, w2, _ in expert_params], jnp.float32)
            logits = x @ router_w + router_b - COST_LAMBDA * cost
            probs = jax.nn.softmax(logits, axis=-1)
            topv, topi = jax.lax.top_k(probs, TOP_K)
            gate = jax.nn.softmax(topv, axis=-1)
            out = jnp.zeros_like(h)
            for k in range(TOP_K):
                mask = jax.nn.one_hot(topi[..., k], E, dtype=h.dtype)
                acc = jnp.zeros_like(h)
                for e, (w1, b1, w2, b2) in enumerate(expert_params):
                    hm = h * mask[..., e:e + 1]
                    acc = acc + (_gelu(_gelu(hm) @ w1 + b1) @ w2 + b2)
                out = out + acc * gate[..., k:k + 1]
            out = out + 0.1 * (_gelu(_gelu(h) @ shared_w1 + shared_b1) @ shared_w2 + shared_b2)
            out = out @ up_w + up_b
            out = out + (_gelu(x) @ core_w + core_b)
            return out
        ep = [(e0_w1, e0_b1, e0_w2, e0_b2), (e1_w1, e1_b1, e1_w2, e1_b2), (e2_w1, e2_b1, e2_w2, e2_b2), (e3_w1, e3_b1, e3_w2, e3_b2), (e4_w1, e4_b1, e4_w2, e4_b2), (e5_w1, e5_b1, e5_w2, e5_b2), (e6_w1, e6_b1, e6_w2, e6_b2), (e7_w1, e7_b1, e7_w2, e7_b2)]
        return _forward(x, down_w, down_b, up_w, up_b, router_w, router_b, shared_w1, shared_b1, shared_w2, shared_b2, core_w, core_b, ep)
    x = x + jnp.tanh(g_xattn[0]) * _L0_xattn_ref(_layernorm(x, axis=-1), ctx_2048, ctx_2048, L0_xattn_gamma)
    x = x + jnp.tanh(g_ffn[0]) * _L0_ffn_ref(_layernorm(x, axis=-1), L0_ffn_down_w, L0_ffn_down_b, L0_ffn_up_w, L0_ffn_up_b, L0_ffn_router_w, L0_ffn_router_b, L0_ffn_shared_w1, L0_ffn_shared_b1, L0_ffn_shared_w2, L0_ffn_shared_b2, L0_ffn_core_w, L0_ffn_core_b, L0_ffn_e0_w1, L0_ffn_e0_b1, L0_ffn_e0_w2, L0_ffn_e0_b2, L0_ffn_e1_w1, L0_ffn_e1_b1, L0_ffn_e1_w2, L0_ffn_e1_b2, L0_ffn_e2_w1, L0_ffn_e2_b1, L0_ffn_e2_w2, L0_ffn_e2_b2, L0_ffn_e3_w1, L0_ffn_e3_b1, L0_ffn_e3_w2, L0_ffn_e3_b2, L0_ffn_e4_w1, L0_ffn_e4_b1, L0_ffn_e4_w2, L0_ffn_e4_b2, L0_ffn_e5_w1, L0_ffn_e5_b1, L0_ffn_e5_w2, L0_ffn_e5_b2, L0_ffn_e6_w1, L0_ffn_e6_b1, L0_ffn_e6_w2, L0_ffn_e6_b2, L0_ffn_e7_w1, L0_ffn_e7_b1, L0_ffn_e7_w2, L0_ffn_e7_b2)
    return x

_drawn_inputs = setup_inputs


def setup_inputs(seed=0):
    import zlib

    import numpy as np

    out = dict(_drawn_inputs(seed))
    spreads = {'L0_ffn_down_b': (0.0, 0.8),
     'L0_ffn_up_b': (0.0, 0.426),
     'L0_ffn_router_b': (0.0, 0.8),
     'L0_ffn_shared_b1': (0.0, 2.0),
     'L0_ffn_shared_b2': (0.0, 2.0),
     'L0_ffn_core_b': (0.0, 0.405),
     'L0_ffn_e0_b1': (0.0, 0.8),
     'L0_ffn_e0_b2': (0.0, 1.325),
     'L0_ffn_e1_b1': (0.0, 0.8),
     'L0_ffn_e1_b2': (0.0, 1.359),
     'L0_ffn_e2_b1': (0.0, 0.8),
     'L0_ffn_e2_b2': (0.0, 1.196),
     'L0_ffn_e3_b1': (0.0, 0.8),
     'L0_ffn_e3_b2': (0.0, 1.304),
     'L0_ffn_e4_b1': (0.0, 0.8),
     'L0_ffn_e4_b2': (0.0, 1.209),
     'L0_ffn_e5_b1': (0.0, 0.8),
     'L0_ffn_e5_b2': (0.0, 1.287),
     'L0_ffn_e6_b1': (0.0, 0.8),
     'L0_ffn_e6_b2': (0.0, 1.216),
     'L0_ffn_e7_b1': (0.0, 0.8),
     'L0_ffn_e7_b2': (0.0, 1.247)}
    factors = {'L0_ffn_down_w': 8.0,
     'L0_ffn_router_w': 8.0,
     'L0_ffn_shared_w1': 8.0,
     'L0_ffn_shared_w2': 8.0,
     'L0_ffn_e0_w1': 8.0,
     'L0_ffn_e0_w2': 8.0,
     'L0_ffn_e1_w1': 8.0,
     'L0_ffn_e1_w2': 8.0,
     'L0_ffn_e2_w1': 8.0,
     'L0_ffn_e2_w2': 7.868,
     'L0_ffn_e3_w1': 8.0,
     'L0_ffn_e3_w2': 7.485,
     'L0_ffn_e4_w1': 8.0,
     'L0_ffn_e4_w2': 8.0,
     'L0_ffn_e5_w1': 8.0,
     'L0_ffn_e5_w2': 8.0,
     'L0_ffn_e6_w1': 8.0,
     'L0_ffn_e6_w2': 7.872,
     'L0_ffn_e7_w1': 8.0,
     'L0_ffn_e7_w2': 7.916}
    for name, (base, spread) in spreads.items():
        noise = np.random.default_rng([zlib.crc32(name.encode()), seed]).standard_normal(out[name].shape)
        drawn = base * np.exp(spread * noise) if base else spread * noise
        out[name] = jnp.asarray(drawn.astype(out[name].dtype))
    for name, factor in factors.items():
        out[name] = (out[name] * factor).astype(out[name].dtype)
    return out
```

```python
from contextlib import ExitStack

import numpy as np

import concourse.bass as bass
from concourse import mybir

F32 = mybir.dt.float32
F16 = mybir.dt.float16
U32 = mybir.dt.uint32
ALU = mybir.AluOpType
ACT = mybir.ActivationFunctionType
AX = mybir.AxisListType

P = 128
B, D, L = 16, 128, 512
NH, DH = 8, 16
QUADS = NH // 2
LB = L // P
SCALE = DH ** -0.5
EPS = 1e-5
HID = [256, 512, 768, 1024, 256, 512, 768, 1024]
E = len(HID)
LAT = 256
NT = sum(HID) // P
COST_LAMBDA = 1e-7
TILES = [h // P for h in HID] + [LAT // P]
FIRST = [sum(TILES[:e]) for e in range(E + 1)]
NTS = sum(TILES)
C_W1 = 0
C_W2 = C_W1 + NTS * LAT
C_DOWN = C_W2 + NTS * LAT
C_CORE = C_DOWN + LB * LAT
C_UP = C_CORE + LB * L
NCOL = C_UP + 2 * L
WCH = NCOL // B
ROWS = 3 * DH
R_ZERO = 65
R_MAX = 65
K_ID, K_M1, K_M2, K_ME, K_MO, K_PH, K_IOTA, K_COST, K_E = 0, 128, 256, 384, 385, 386, 388, 396, 428
NCONST = 460


class Tally:

    def __init__(self, sem, step=1):
        self.sem, self.step, self.value, self.at = sem, step, 0, {}

    def plan(self, *key, n=1):
        self.value += self.step * n
        self.at[key] = self.value


class Clock:

    def __init__(self, eng, period, setup, apart=False):
        self.eng, self.turn, self.period, self.setup = eng, None, period, setup
        self.apart = apart

    def wait(self, tally, *key, apart=False):
        if key not in tally.at:
            assert self.turn is None and key[0] < 0
            return
        v = tally.at[key]
        if self.turn is not None:
            later = (key[0] + self.period,) + key[1:]
            v = v + self.turn * (tally.at[later] - v)
            if apart or self.apart:
                v = self.eng.to_reg(v)
                self.eng.wait_ge(self.setup.sem, self.setup.value)
        self.eng.wait_ge(tally.sem, v)

    def index(self, n):
        return n if self.turn is None else n + self.turn * self.period


def pack(inputs):
    f = lambda a: np.asarray(a)
    kt = lambda w: f(w).reshape(-1, P, f(w).shape[1]).transpose(1, 0, 2)
    g = lambda n: inputs["L0_ffn_" + n]
    experts = [f"e{e}_" for e in range(E)] + ["shared_"]
    w1 = [kt(g(n + "w1")).reshape(P, 2, -1, P).transpose(0, 2, 1, 3).reshape(P, -1) for n in experts]
    w2 = [kt(g(n + "w2")).reshape(P, -1) for n in experts]
    rest = [kt(g(n)).reshape(P, -1) for n in ("down_w", "core_w", "up_w")]
    wall = np.ascontiguousarray(np.concatenate(w1 + w2 + rest, 1))
    col = lambda n: f(g(n)).reshape(-1, P).T
    bcol = np.ascontiguousarray(np.concatenate(
        [col(n + "b1") for n in experts] + [col("down_b")], 1))
    b2 = np.zeros((P, LAT), np.float32)
    for e in range(E):
        b2[e] = f(g(f"e{e}_b2"))
    b2[E] = f(g("shared_b2"))
    rw = np.zeros((P, LB, 32), np.float32)
    rw[:, :, :E] = kt(g("router_w"))
    return wall, bcol, b2, rw


def constants():
    c = np.zeros((P, NCONST), np.float32)
    c[:, K_ID:K_ID + P] = np.eye(P)
    for q in range(4):
        c[32 * q:32 * q + E, K_M1:K_M1 + E] = 1 - np.eye(E)
    c[0:E, K_M2:K_M2 + E] = 1
    c[E, K_M2 + E] = 0.1
    even = (np.arange(P) % 32) < DH
    c[:, K_ME], c[:, K_MO] = even, ~even
    c[:, K_PH] = -0.5
    c[:, K_IOTA:K_IOTA + E] = np.arange(E)
    c[:, K_COST:K_COST + 4 * E] = np.tile(np.float32(COST_LAMBDA) * np.array([2 * LAT * h for h in HID], np.float32), 4)
    c[:, K_E:K_E + 4 * E] = np.e
    return c


def program(nc, x, ctx_kv, gx, gf, gamma, wall, bcol, b2, rw, rb, upb, coreb, const, ones, out, upto=2):
    att = nc.dram_tensor("att_scratch", [B, P, L], F32, kind="Internal").ap()
    sq = nc.dram_tensor("q_scratch", [B, 2, P, L], F16, kind="Internal").ap()
    sk = nc.dram_tensor("k_scratch", [B, 2, P, L], F16, kind="Internal").ap()
    sd = nc.dram_tensor("den_scratch", [B, 2, NH, L], F32, kind="Internal").ap()
    with ExitStack() as whole:
        sb = lambda n, s, d=F32, c=whole: c.enter_context(nc.sbuf_tensor(n, s, d))
        ps = lambda n, s, c=whole: c.enter_context(nc.psum_tensor(n, s, F32))
        sem = lambda n: whole.enter_context(nc.semaphore(n))
        keep = {
            "cst": sb("cst", [P, NCONST]), "whi": sb("whi", [P, NCOL], F16), "wlo": sb("wlo", [P, NCOL], F16),
            "gate": sb("gate", [P, 6]),
        }
        with ExitStack() as c:
            attention(nc, c, keep, sb, ps, sem, x, ctx_kv, gx, gf, gamma, wall, const, ones,
                      att if upto == 2 else out, sq, sk, sd)
        if upto == 2:
            with ExitStack() as c:
                ffn(nc, c, keep, sb, ps, sem, x, att, bcol, b2, rw, rb, upb, coreb, out)


def attention(nc, c, keep, sb, ps, sem, x, ctx_kv, gx, gf, gamma, wall, const, ones, att, sq, sk, sd):
    cst, whi, wlo, gate = keep["cst"], keep["whi"], keep["wlo"], keep["gate"]
    ident = cst[:, K_ID:K_ID + P]
    A = lambda n, s, d=F32: sb(n, s, d, c)
    xt = [A(f"xt{i}", [P, L]) for i in range(2)]
    ct = [A(f"ct{i}", [P, L]) for i in range(2)]
    wst = [A(f"wst{i}", [P, WCH]) for i in range(2)]
    stats, mv = A("stats", [P, 6]), [A(f"mv{i}", [P, 2]) for i in range(2)]
    ln = [A(f"ln{i}", [P, 4]) for i in range(2)]
    qf = A("qf", [P, L])
    qhl = [A(f"qhl{i}", [P, 2, L], F16) for i in range(2)]
    khl = [A(f"khl{i}", [P, 2, L], F16) for i in range(2)]
    QS = [A(f"QS{i}", [R_MAX + 1, 2, QUADS, L], F16) for i in range(2)]
    KS = [A(f"KS{i}", [R_MAX + 1, 2, QUADS, L], F16) for i in range(2)]
    VT = [A(f"VT{i}", [P, LB, 2, QUADS, 32]) for i in range(2)]
    mx = A("mx", [P, 32])
    mrow = A("mrow", [16, P], F16)
    Pb = [A(f"P{i}", [P, L]) for i in range(8)]
    U = [A(f"U{g}", [P, L]) for g in range(2)]
    tn, t2 = A("tn", [P, L]), A("t2", [P, L])
    cme = A("cme", [P, 2])
    dc, rc = A("dc", [P, NH * L // P]), A("rc", [P, NH * L // P])
    rd = A("rd", [P, L])
    ao = [A(f"ao{i}", [P, L]) for i in range(2)]
    nat = [ps(f"nat{i}", [P, 2, L], c) for i in range(2)]
    ring = [ps(f"ring{i}", [P, L], c) for i in range(3)]
    pv = ps("pv", [P, L], c)

    T = lambda n, step=1: Tally(sem(n), step)
    t_cst, t_one, t_set, t_vt, t_gate = T("a_cst", 16), T("a_ones", 16), T("a_set"), T("a_vt"), T("a_gate")
    t_x, t_c, t_wl = ([T(f"{n}_in{i}", 16) for i in range(2)] for n in ("x", "ctx", "w"))
    t_sq, t_sk = T("q_out", 16), T("k_out", 16)
    t_stk = [T(f"stack_in{g}", 16) for g in range(2)]
    t_m = [T(f"max_row_in{g}", 16) for g in range(2)]
    t_ds, t_dc, t_rs, t_rb = T("den_out", 16), T("den_in", 16), T("recip_out", 16), T("recip_in", 16)
    t_st = T("att_out", 16)
    t_nat, t_ring, t_pv = T("pe_nat"), T("pe_ring"), T("pe_pv")
    t_use, t_ev = T("act_ring"), T("act_evac")
    t_wh = T("act_whi")
    t_max, t_dve, t_pool = T("dve_max"), T("dve_small"), T("pool")

    t_cst.plan("all", n=4)
    def pe_jobs(w):
        t = w - 1
        jobs = []
        for s in range(8):
            for half in range(2):
                if w < B:
                    jobs.append(("nat", w, 2 * s + half))
                if 0 <= t < B:
                    jobs += [("st", t, s, 2 * half), ("st", t, s, 2 * half + 1)]
            if 0 <= t < B and s:
                jobs.append(("pv", t, s - 1))
            if s == 0 and 0 <= t - 1:
                jobs.append(("pv", t - 1, 7))
            if s == 0 and 0 <= t < B:
                jobs.append(("m", t, 1))
            if s == 1 and w < B:
                jobs += [("vt", w, 0), ("vt", w, 1)]
            if s == 4 and w < B:
                jobs.append(("m", w, 0))
            if w == B + 1:
                break
        return jobs

    WINDOWS = range(B + 2)
    ring_keys = []
    for w in WINDOWS:
        for kind, *key in pe_jobs(w):
            if kind == "nat":
                t_nat.plan(*key); t_max.plan(*key)
            elif kind == "pv":
                t_pv.plan(*key)
                if key[1] % 4 == 3:
                    t_ev.plan(key[0], key[1] // 4)
            else:
                k = (key[0], kind, *key[1:])
                ring_keys.append(k)
                t_ring.plan(*k); t_use.plan(*k)
    place = {k: n for n, k in enumerate(ring_keys)}

    def dve_small(w):
        return ([(w + 1, "stats"), (w + 1, "aggr")] if w + 1 < B else []) + \
               ([(w - 2, "recip")] if w >= 2 else [])

    def pool_jobs(w):
        jobs = []
        if w + 1 < B:
            jobs += [(w + 1, n) for n in ("kh", "kl", "negm", "veps", "rstd", "rs", "qf", "qh", "ql")]
        if w >= 2:
            jobs += [(w - 2, n) for n in ("na", "nb", "num")]
        if 0 <= w < B:
            jobs += [(w, "wlo")]
        if w >= 2:
            jobs += [(w - 2, "att")]
        return jobs

    for w in range(-1, B + 2):
        for k in dve_small(w):
            t_dve.plan(*k)
        for k in pool_jobs(w):
            t_pool.plan(*k)
        if w + 1 < B:
            for t_ in (t_x[(w + 1) % 2], t_c[(w + 1) % 2], t_sq, t_sk):
                t_.plan(w + 1)
            for g in range(2):
                t_stk[g].plan(w + 1, n=6)
        if 0 <= w < B:
            t_wl[w % 2].plan(w)
            t_wh.plan(w)
            for g in range(2):
                t_m[g].plan(w)
        if w >= 2:
            t_ds.plan(w - 2, n=2)
            t_rb.plan(w - 2)
            for t_ in (t_dc, t_rs, t_st):
                t_.plan(w - 2)

    def over_windows(eng, body, apart=False):
        ck = Clock(eng, 2, t_cst, apart)
        for w in range(-1, 4):
            body(ck, w)
        with eng.Fori(0, (B - 6) // 2) as turn:
            ck.turn = turn
            body(ck, 4)
            body(ck, 5)
        ck.turn = None
        for w in range(B - 2, B + 2):
            body(ck, w)

    block = c.enter_context(nc.Block())

    @block.sync
    def _(sp):
        for dst, src in ((cst[:, :], const), (gate[:, 0:1], gx.partition_broadcast(P)), (gate[:, 1:2], gf.partition_broadcast(P)),
                         (gate[:, 2:3], gamma.partition_broadcast(P))):
            sp.dma_start(dst, src).then_inc(t_cst.sem, 16)
        sp.wait_ge(t_set.sem, 4)
        for i in range(2):
            sp.dma_start(KS[i][R_MAX:R_MAX + 1, :, :, :].rearrange("o g j q -> o (g j q)"), ones).then_inc(t_one.sem, 16)

        def max_row(ck, b, g):
            ck.wait(t_use, b, "m", g)
            sp.dma_start(QS[b % 2][R_MAX:R_MAX + 1, g, :, :].rearrange("o j q -> o (j q)").rearrange("o (r p) -> o r p", p=P),
                         mrow[:, :]).then_inc(t_m[g].sem, 16)

        def stack(ck, b, g):
            ck.wait(t_ring, b - 2, "st", 4 * g + 3, 3)
            for scr, dst, parts in ((sq, QS[b % 2], (0, 1, 0)), (sk, KS[b % 2], (0, 0, 1))):
                for n, part in enumerate(parts):
                    src = scr[ck.index(b), part].rearrange("(j g d) q -> g d j q", g=2, d=DH)[g]
                    sp.dma_start(dst[DH * n:DH * n + DH, g, :, :], src).then_inc(t_stk[g].sem, 16)

        def load_x(ck, b):
            ck.wait(t_pool, b - 2, "qf")
            sp.dma_start(xt[b % 2][:, :], x[ck.index(b)]).then_inc(t_x[b % 2].sem, 16)

        def load_ctx(ck, b):
            ck.wait(t_pool, b - 2, "kl")
            ck.wait(t_ring, b - 2, "vt", 1)
            sp.dma_start(ct[b % 2][:, :], ctx_kv[ck.index(b)]).then_inc(t_c[b % 2].sem, 16)

        def load_weights(ck, n):
            ck.wait(t_pool, n - 2, "wlo")
            sp.dma_start(wst[n % 2][:, :], wall[:, bass.ds(ck.index(n) * WCH, WCH)]).then_inc(t_wl[n % 2].sem, 16)

        def body(ck, w):
            b, t = w + 1, w - 2
            if w < 0:
                for n in range(2):
                    load_x(ck, n)
                    load_ctx(ck, n)
                load_weights(ck, 0)
            if 1 <= w <= B:
                max_row(ck, w - 1, 1)
            if 0 <= w < B - 2:
                load_x(ck, w + 2)
            if 0 <= w < B - 1:
                load_weights(ck, w + 1)
            if t >= 0:
                ck.wait(t_ev, t, 1)
                for g in range(2):
                    r = DH * (1 - g)
                    sp.dma_start(sd[ck.index(t), 0].rearrange("(j g) q -> g j q", g=2)[g], U[g][r:P:32, :]).then_inc(t_ds.sem, 16)
            if 0 <= w < B - 2:
                load_ctx(ck, w + 2)
            if t >= 0:
                ck.wait(t_ds, t)
                ck.wait(t_dve, t - 1, "recip")
                sp.dma_start(dc[:, :], sd[ck.index(t), 0].rearrange("h (s q) -> (h s) q", s=P // NH)).then_inc(t_dc.sem, 16)
            if b < B:
                ck.wait(t_pool, b, "kl")
                sp.dma_start(sk[ck.index(b)].rearrange("t p q -> p t q"), khl[b % 2][:, :, :]).then_inc(t_sk.sem, 16)
                ck.wait(t_pool, b, "ql")
                sp.dma_start(sq[ck.index(b)].rearrange("t p q -> p t q"), qhl[b % 2][:, :, :]).then_inc(t_sq.sem, 16)
            if t >= 0:
                ck.wait(t_dve, t, "recip")
                sp.dma_start(sd[ck.index(t), 1].rearrange("h (s q) -> (h s) q", s=P // NH), rc[:, :]).then_inc(t_rs.sem, 16)
            if b < B:
                ck.wait(t_sq, b)
                ck.wait(t_sk, b)
                stack(ck, b, 0)
            if t >= 0:
                ck.wait(t_rs, t)
                ck.wait(t_pool, t - 1, "att")
                sp.dma_start(rd[:, :], sd[ck.index(t), 1].unsqueeze(1).broadcast_to([NH, DH, L])).then_inc(t_rb.sem, 16)
            if 0 <= w < B:
                max_row(ck, w, 0)
            if t >= 0:
                ck.wait(t_pool, t, "att")
                sp.dma_start(att[ck.index(t)], ao[t % 2][:, :]).then_inc(t_st.sem, 16)
            if b < B:
                stack(ck, b, 1)

        over_windows(sp, body, apart=True)
        sp.wait_ge(t_st.sem, t_st.value)

    @block.tensor
    def _(pe):
        pe.wait_ge(t_cst.sem, 16 * 4)
        pe.wait_ge(t_one.sem, 16 * 2)

        def ring_free(ck, key):
            n = place[key] - 3
            if n >= 0:
                ck.wait(t_use, *ring_keys[n])

        def body(ck, w):
            if w < 0:
                return
            for kind, b, *rest in pe_jobs(w):
                i = b % 2
                if kind == "nat":
                    k, = rest
                    g, j = k // 8, k % 8 // 2
                    if k % 8 == 0:
                        ck.wait(t_stk[g], b)
                    ck.wait(t_max, *((b, k - 2) if k >= 2 else (b - 1, k + 14)))
                    for h in range(2):
                        q0 = (2 * (k % 2) + h) * P
                        m = pe.matmul(nat[k % 2][:, h, :], QS[i][0:R_ZERO, g, j, q0:q0 + P], KS[i][0:R_ZERO, g, j, :],
                                      start=True, stop=True)
                    m.then_inc(t_nat.sem, 1)
                elif kind == "st":
                    s, j = rest
                    g, lb = s // 4, s % 4
                    if lb == 0 and j == 0:
                        ck.wait(t_m[g], b)
                    key = (b, "st", s, j)
                    ring_free(ck, key)
                    pe.matmul(ring[place[key] % 3][:, :], KS[i][0:R_MAX + 1, g, j, lb * P:lb * P + P],
                              QS[i][0:R_MAX + 1, g, j, :], start=True, stop=True).then_inc(t_ring.sem, 1)
                elif kind == "pv":
                    s, = rest
                    g, lb = s // 4, s % 4
                    if s == 0:
                        ck.wait(t_use, b, "vt", 1)
                    if lb == 0:
                        ck.wait(t_ev, *((b, 0) if g else (b - 1, 1)))
                    ck.wait(t_use, b, "st", s, 3)
                    for j in range(QUADS):
                        m = pe.matmul(pv[32 * j:32 * j + 32, :], VT[i][:, lb, g, j, :], Pb[4 * (s % 2) + j][:, :],
                                      start=(lb == 0), stop=(lb == 3))
                    m.then_inc(t_pv.sem, 1)
                elif kind == "m":
                    g, = rest
                    key = (b, "m", g)
                    ck.wait(t_max, b, 8 * g + 7)
                    ring_free(ck, key)
                    pe.transpose(ring[place[key] % 3][0:16, 0:P], mx[:, 16 * g:16 * g + 16], ident).then_inc(t_ring.sem, 1)
                else:
                    a, = rest
                    key = (b, "vt", a)
                    if a == 0:
                        ck.wait(t_c[b % 2], b)
                    ring_free(ck, key)
                    for n in range(2):
                        lb = 2 * a + n
                        m = pe.transpose(ring[place[key] % 3][:, n * P:n * P + P], ct[i][:, lb * P:lb * P + P], ident)
                    m.then_inc(t_ring.sem, 1)

        over_windows(pe, body)

    @block.scalar
    def _(act):
        act.wait_ge(t_cst.sem, 16 * 4)
        act.activation(gate[:, 3:5], gate[:, 0:2], ACT.Tanh).then_inc(t_gate.sem, 1)
        act.wait_ge(t_vt.sem, 2)

        def body(ck, w):
            if w < 0:
                return
            for kind, b, *rest in pe_jobs(w):
                i = b % 2
                if kind == "nat":
                    if rest[0] == 10:
                        ck.wait(t_wl[w % 2], w)
                        act.copy(whi[:, bass.ds(ck.index(w) * WCH, WCH)], wst[w % 2][:, :]).then_inc(t_wh.sem, 1)
                    continue
                if kind == "pv":
                    s, = rest
                    if s % 4 == 3:
                        g = s // 4
                        ck.wait(t_pv, b, s)
                        ck.wait(t_pool, b - 1, "nb")
                        ck.wait(t_ds, b - 1)
                        act.copy(U[g][:, :], pv[:, :]).then_inc(t_ev.sem, 1)
                    continue
                key = (b, kind, *rest)
                bank = ring[place[key] % 3]
                ck.wait(t_ring, *key)
                if kind == "st":
                    s, j = rest
                    if j == 0:
                        ck.wait(t_pv, *((b, s - 2) if s >= 2 else (b - 1, s + 6)))
                    act.activation(Pb[4 * (s % 2) + j][:, :], bank[:, :], ACT.Exp).then_inc(t_use.sem, 1)
                elif kind == "m":
                    g, = rest
                    if g == 1:
                        ck.wait(t_m[0], b)
                    else:
                        ck.wait(t_m[1], b - 1)
                    act.mul(mrow[:, :], bank[0:16, 0:P], -1.0).then_inc(t_use.sem, 1)
                else:
                    a, = rest
                    src = bank[:, 0:2 * P].rearrange("p (l j g d) -> p l g j d", l=2, g=2, d=DH)
                    for g in range(2):
                        m = act.copy(VT[i][:, 2 * a:2 * a + 2, g, :, DH * g:DH * g + DH], src[:, :, g, :, :])
                    m.then_inc(t_use.sem, 1)

        over_windows(act, body)

    @block.vector
    def _(dve):
        for i in range(2):
            dve.memset(QS[i][:, :, :, :], 0.0).then_inc(t_set.sem, 1)
            dve.memset(KS[i][:, :, :, :], 0.0).then_inc(t_set.sem, 1)

        def small(ck, b, what):
            i = b % 2
            if what == "stats":
                ck.wait(t_x[b % 2], b)
                dve.bn_stats(stats[:, :], xt[i][:, :]).then_inc(t_dve.sem, 1)
            elif what == "aggr":
                ck.wait(t_dve, b, "stats", apart=True)
                dve.bn_aggr(mv[i][:, :], stats[:, :]).then_inc(t_dve.sem, 1)
            else:
                ck.wait(t_dc, b)
                ck.wait(t_rs, b - 1)
                dve.reciprocal(rc[:, :], dc[:, :]).then_inc(t_dve.sem, 1)

        def body(ck, w):
            todo = dve_small(w)
            if 0 <= w < B:
                for k in range(16):
                    ck.wait(t_nat, w, k)
                    dve.tensor_reduce(mx[:, 2 * k:2 * k + 2], nat[k % 2][:, :, :], AX.X, ALU.max).then_inc(t_max.sem, 1)
                    if todo and (k in (1, 2) and todo[0][1] != "recip" or k == 7):
                        small(ck, *todo.pop(0))
            for job in todo:
                small(ck, *job)

        over_windows(dve, body)

    @block.gpsimd
    def _(pool):
        for i in range(2):
            pool.memset(VT[i][:, :, :, :, :], 1.0).then_inc(t_vt.sem, 1)
        pool.wait_ge(t_cst.sem, 16 * 4)
        pool.wait_ge(t_gate.sem, 1)
        pool.tensor_tensor(gate[:, 5:6], gate[:, 3:4], gate[:, 2:3], ALU.mult).then_inc(t_gate.sem, 1)
        pool.wait_ge(t_gate.sem, 2)
        pool.tensor_scalar(cme[:, 0:2], cst[:, K_ME:K_ME + 2], gate[:, 5:6], None, ALU.mult).then_inc(t_gate.sem, 1)
        pool.wait_ge(t_gate.sem, 3)

        def job(ck, b, what):
            i = b % 2
            done = lambda ins: ins.then_inc(t_pool.sem, 1)
            v, m = ln[i], mv[i]
            if what == "na":
                ck.wait(t_ev, b, 1)
                ck.wait(t_pool, b - 1, "att")
                done(pool.tensor_scalar(tn[:, :], U[0][:, :], cme[:, 0:1], 1.0, ALU.mult, ALU.mult))
            elif what == "nb":
                done(pool.tensor_scalar(t2[:, :], U[1][:, :], cme[:, 1:2], 1.0, ALU.mult, ALU.mult))
            elif what == "num":
                ck.wait(t_pool, b, "nb")
                done(pool.tensor_tensor(tn[:, :], tn[:, :], t2[:, :], ALU.add))
            elif what == "att":
                ck.wait(t_rb, b)
                ck.wait(t_pool, b, "num")
                ck.wait(t_st, b - 2)
                done(pool.tensor_tensor(ao[i][:, :], tn[:, :], rd[:, :], ALU.mult))
            elif what == "negm":
                ck.wait(t_dve, b, "aggr")
                done(pool.tensor_scalar(v[:, 0:1], m[:, 0:1], -1.0, None, ALU.mult))
            elif what == "veps":
                done(pool.tensor_scalar(v[:, 1:2], m[:, 1:2], EPS, None, ALU.add))
            elif what == "rstd":
                ck.wait(t_pool, b, "veps")
                done(pool.tensor_tensor(v[:, 2:3], v[:, 1:2], cst[:, K_PH:K_PH + 1], ALU.pow))
            elif what == "rs":
                ck.wait(t_pool, b, "rstd")
                done(pool.tensor_scalar(v[:, 3:4], v[:, 2:3], SCALE, None, ALU.mult))
            elif what == "qf":
                ck.wait(t_pool, b, "rs")
                done(pool.tensor_scalar(qf[:, :], xt[i][:, :], v[:, 0:1], v[:, 3:4], ALU.add, ALU.mult))
            elif what == "qh":
                ck.wait(t_pool, b, "qf")
                ck.wait(t_sq, b - 2)
                done(pool.tensor_scalar(qhl[i][:, 0, :], qf[:, :], 1.0, 1.0, ALU.mult, ALU.mult))
            elif what == "ql":
                ck.wait(t_pool, b, "qh")
                done(pool.tensor_tensor(qhl[i][:, 1, :], qf[:, :], qhl[i][:, 0, :], ALU.subtract))
            elif what == "kh":
                ck.wait(t_c[b % 2], b)
                ck.wait(t_sk, b - 2)
                done(pool.tensor_scalar(khl[i][:, 0, :], ct[i][:, :], 1.0, 1.0, ALU.mult, ALU.mult))
            elif what == "kl":
                ck.wait(t_pool, b, "kh")
                done(pool.tensor_tensor(khl[i][:, 1, :], ct[i][:, :], khl[i][:, 0, :], ALU.subtract))
            elif what == "wlo":
                ck.wait(t_wh, b)
                cols = bass.ds(ck.index(b) * WCH, WCH)
                done(pool.tensor_tensor(wlo[:, cols], wst[i][:, :], whi[:, cols], ALU.subtract))

        def body(ck, w):
            for k in pool_jobs(w):
                job(ck, *k)

        over_windows(pool, body, apart=True)



ORDER = [3, 7, E, 2, 6, 1, 5, 0, 4]
SEQ = [(e, n) for e in ORDER for n in range(TILES[e])]
G4 = 4
NG = B // G4


def ffn(nc, c, keep, sb, ps, sem, x, att, bcol, b2, rw, rb, upb, coreb, out):
    cst, whi, wlo, gate = keep["cst"], keep["whi"], keep["wlo"], keep["gate"]
    ident = cst[:, K_ID:K_ID + P]
    A = lambda n, s, d=F32: sb(n, s, d, c)
    bc, b2s, rws = A("bc", [P, NTS + 2]), A("b2s", [P, LAT]), A("rws", [P, LB, 32])
    rbb, tb, tb2 = A("rbb", [P, G4, E]), A("tb", [P, L]), A("tb2", [P, L])
    gb, gbh, gbl = A("gb", [P, NT]), A("gbh", [P, NT, 32], F16), A("gbl", [P, NT, 32], F16)
    zs, Z = A("zs", [P, LAT]), A("Z", [P, LAT])
    X, XA, XB = A("X", [P, G4, L]), A("XA", [P, G4, L]), A("XB", [P, G4, L])
    st, mv, lnv = A("st4", [P, G4, 6]), A("mv4", [P, G4, 2]), A("ln4", [P, 2, G4])
    u = A("u", [P, G4, L])
    uf = A("uf", [P, LB, L])
    uh, ul = A("uh", [P, LB, L], F16), A("ul", [P, LB, L], F16)
    guh, gul = A("guh", [P, LB, L], F16), A("gul", [P, LB, L], F16)
    gf_, gh, gl = A("gf", [P, 2, L]), A("gh", [P, 2, L], F16), A("gl", [P, 2, L], F16)
    lp = A("lp", [P, L])
    lg, pe_, pp, t8, t8i = A("lg", [P, G4, E]), A("pexp", [P, G4, E]), A("pp", [P, G4, E]), A("top", [P, G4, 8]), A("topi", [P, G4, 8], U32)
    red = A("red", [P, 8, G4])
    tif, m1, m2 = A("tif", [P, G4, 2]), A("m1", [P, G4, E]), A("m2", [P, G4, E])
    Gp, GT = A("Gp", [P, G4, P]), A("GT", [P, L])
    af = [A(f"af{i}", [P, L]) for i in range(3)]
    ah = [A(f"ah{i}", [P, L], F16) for i in range(3)]
    al = [A(f"al{i}", [P, L], F16) for i in range(3)]
    acc = A("acc", [P, G4, LAT])
    oh, ol = A("oh", [P, 2, L], F16), A("ol", [P, 2, L], F16)
    H = [ps(f"H{i}", [P, L], c) for i in range(4)]
    Y = [ps(f"Y{i}", [P, G4, LAT], c) for i in range(2)]

    T = lambda n, step=1: Tally(sem(n), step)
    t_in, t_xx, t_o = T("f_in", 16), T("f_x", 16), T("f_out", 16)
    t_in.plan("all", n=6)
    t_pe, t_act, t_dve, t_pool = T("f_pe"), T("f_act"), T("f_dve"), T("f_pool")

    NA = len(SEQ)
    LAG = 2
    ring = ([("uT", k) for k in range(LB)] + [("lg", 0), ("h", 0), ("h", 1), ("lt", 0)] +
            [("a", 0), ("a", 1), ("a", 2), ("a", 3), ("gt", 0)] + [("a", n) for n in range(4, NA)] +
            [("fin", 0), ("fin", 1), ("ot", 0), ("ot", 1), ("fin", 2), ("fin", 3)])
    bank = {k: n % 4 for n, k in enumerate(ring)}
    ACT_EMPTIES = ("uT", "lg", "h", "a", "gt")

    def y_last(e):
        return SEQ.index((e, TILES[e] - 1))

    pe_ops = [("uT", k) for k in range(LB)] + [("lg", 0), ("h", 0), ("h", 1), ("lt", 0)]
    for n in range(NA + LAG):
        if n < NA:
            pe_ops.append(("a", n))
        if n == 3:
            pe_ops.append(("gt", 0))
        if n >= LAG:
            pe_ops.append(("y", n - LAG))
    pe_ops += [("core", 0), ("core", 1), ("ot", 0), ("ot", 1), ("fin", 0), ("fin", 1), ("core", 2), ("fin", 2), ("core", 3), ("fin", 3)]

    act_ops = [("uT", k) for k in range(LB)] + [("lg", 0), ("h", 0), ("h", 1)]
    for n in range(NA):
        act_ops.append(("a", n))
        if n in (4, 6, 8, 10):
            act_ops.append(("gu", (n - 4) // 2))
        if n == 3:
            act_ops.append(("gt", 0))
    act_ops += [("ot", 0), ("ot", 1)]

    router = ["lred", "lb", "lmx", "lsub", "psum", "prcp", "pp"] + [f"max{t}" for t in range(G4)] + \
             [f"idx{t}" for t in range(G4)] + ["tif", "dz", "e1", "g1", "g2", "m1", "m2", "G1", "G2", "G"]
    dve_ops = [("ul", k) for k in range(LB)] + [("gl", 0), ("gl", 1)] + [("r", n) for n in router[:4]]
    rest = [("r", n) for n in router[4:]]
    for n in range(NA):
        dve_ops.append(("al", n))
        if n == 0:
            dve_ops += rest
        if n in (5, 7, 9, 11):
            dve_ops.append(("gul", (n - 5) // 2))
        if n >= 3 and SEQ[n - 3][1] == TILES[SEQ[n - 3][0]] - 1:
            dve_ops += [("acc", SEQ[n - 3][0], t) for t in range(G4)]
        if n == 24:
            dve_ops += [("stats", t) for t in range(G4)] + [("aggr", t) for t in range(G4)]
    done = {o[1] for o in dve_ops if o[0] == "acc"}
    dve_ops += [("acc", e, t) for e in ORDER if e not in done for t in range(G4)]
    dve_ops += [("ot", 0), ("ot", 1)] + [("fin", t) for t in range(G4)]

    pool_ops = [("uh", k) for k in range(LB)] + [("gh", 0), ("gh", 1)]
    for n in range(NA):
        if n == 1:
            pool_ops.append(("pexp", 0))
        pool_ops.append(("ah", n))
        if n == 2:
            pool_ops.append(("e2", 0))
        if n in (5, 7, 9, 11):
            pool_ops.append(("guh", (n - 5) // 2))
        if n in (13, 14, 15, 16):
            pool_ops.append(("xb", n - 13))
        if n in (20, 21, 22, 23):
            pool_ops.append(("x1", n - 20))
        if n == 25:
            pool_ops += [("negm", 0), ("rstd", 0), ("rstd", 1)]
        if n in (26, 27, 28, 29):
            pool_ops.append(("u", n - 26))
    FRONT = ("x1", "stats", "aggr", "negm", "rstd", "u")

    def of_group(ops, r):
        for name, *i in ops:
            if name in FRONT:
                if r + 1 < NG:
                    yield (r + 1, name, *i)
            elif r >= 0:
                yield (r, name, *i)

    for r in range(-1, NG):
        for tally, ops in ((t_pe, pe_ops), (t_act, act_ops), (t_dve, dve_ops), (t_pool, pool_ops)):
            for k in of_group(ops, r):
                tally.plan(*k)
        if r + 1 < NG:
            t_xx.plan(r + 1, n=2)
        if r >= 0:
            t_o.plan(r, n=G4)
    t_z, t_zd, t_zp = T("f_z"), T("f_zd"), T("f_zp")

    def over_groups(eng, ops, do, apart=False):
        ck = Clock(eng, 1, t_in, apart)
        for k in of_group(ops, -1):
            do(ck, *k)
        for k in of_group(ops, 0):
            do(ck, *k)
        with eng.Fori(0, NG - 2) as turn:
            ck.turn = turn
            for k in of_group(ops, 1):
                do(ck, *k)
        ck.turn = None
        for k in of_group(ops, NG - 1):
            do(ck, *k)

    block = c.enter_context(nc.Block())

    @block.sync
    def _(sp):
        for dst, src in ((bc[:, :], bcol), (b2s[:, :], b2), (rws[:, :, :], rw), (tb[:, :], upb.partition_broadcast(P)),
                         (tb2[:, :], coreb.partition_broadcast(P)),
                         (rbb[:, :, :], rb.unsqueeze(0).broadcast_to([G4, E]).partition_broadcast(P))):
            sp.dma_start(dst, src).then_inc(t_in.sem, 16)

        def loads(ck, r):
            for t in range(G4):
                ck.wait(t_pool, r - 1, "xb", t)
            ck.wait(t_dve, r - 1, "stats", G4 - 1)
            ck.wait(t_pool, r - 1, "u", G4 - 1)
            rows = bass.ds(ck.index(r) * G4, G4)
            sp.dma_start(X[:, :, :], x[rows].rearrange("t p q -> p t q")).then_inc(t_xx.sem, 16)
            sp.dma_start(XA[:, :, :], att[rows].rearrange("t p q -> p t q")).then_inc(t_xx.sem, 16)

        def body(ck, r):
            if r + 1 < NG:
                loads(ck, r + 1)
            for t in range(G4):
                ck.wait(t_dve, r, "fin", t)
                sp.dma_start(out[ck.index(r) * G4 + t], XB[:, t, :]).then_inc(t_o.sem, 16)

        ck = Clock(sp, 1, t_in, apart=True)
        loads(ck, 0)
        body(ck, 0)
        with sp.Fori(0, NG - 2) as turn:
            ck.turn = turn
            body(ck, 1)
        ck.turn = None
        body(ck, NG - 1)
        sp.wait_ge(t_o.sem, t_o.value)

    @block.tensor
    def _(pe):
        def three(dst, w, wc, mh, ml, first, last, swap=False, skip=False):
            terms = ((whi, mh), (wlo, mh), (whi, ml)) if not swap else ((whi, mh), (wlo, mh), (whi, ml))
            for n, (a, b) in enumerate(terms):
                l, r = (b, a[:, wc]) if swap else (a[:, wc], b)
                m = pe.matmul(dst, l, r, start=first and n == 0, stop=last and n == 2, skip_group_check=skip)
            return m

        pe.wait_ge(t_z.sem, 3)
        for n in range(NT):
            q = n % 4
            wc = slice(C_W2 + n * LAT, C_W2 + (n + 1) * LAT)
            for k, (g_, w_) in enumerate(((gbh, whi), (gbl, whi), (gbh, wlo))):
                m = pe.matmul(Y[0][32 * q:32 * q + 32, 0, :], g_[:, n, :], w_[:, wc],
                              start=(n < 4 and k == 0), stop=(n >= NT - 4 and k == 2))
        m.then_inc(t_z.sem, 1)
        pe.wait_ge(t_z.sem, 5)
        pe.matmul(Y[1][:, 0, :], cst[:, K_M1:K_M1 + P], zs[:, :], start=True, stop=False)
        pe.matmul(Y[1][:, 0, :], cst[:, K_M2:K_M2 + P], b2s[:, :], start=False, stop=True).then_inc(t_z.sem, 1)

        def do(ck, r, name, i):
            key = (name, i) if name != "core" else ("fin", i)
            if key in bank and not (name == "fin"):
                p = ring.index(key)
                if p >= 4:
                    prev, pr = ring[p - 4], r
                else:
                    prev = [k for k in ring if bank[k] == bank[key]][-1]
                    pr = r - 1
                t_ = t_act if prev[0] in ACT_EMPTIES else t_dve
                if prev[0] == "lt":
                    prev = ("r", "lred")
                ck.wait(t_, pr, *prev)
            if name != "y":
                dst = H[bank[key]]
            if name == "uT":
                if i == 0:
                    for t in range(G4):
                        ck.wait(t_pool, r, "u", t)
                for t in range(G4):
                    m = pe.transpose(dst[:, t * P:t * P + P], u[:, t, i * P:i * P + P], ident)
            elif name == "lg":
                for k in range(LB):
                    ck.wait(t_act, r, "uT", k)
                    m = pe.matmul(dst[32 * k:32 * k + 32, :], rws[:, k, :], uf[:, k, :], start=True, stop=True)
            elif name == "lt":
                ck.wait(t_act, r, "lg", 0)
                for t in range(G4):
                    m = pe.transpose(dst[:, t * P:t * P + P], lp[:, t * P:t * P + P], ident)
            elif name == "h":
                for k in range(LB):
                    if i == 0:
                        ck.wait(t_pool, r, "uh", k)
                        ck.wait(t_dve, r, "ul", k)
                    c0 = C_DOWN + k * LAT + i * P
                    m = three(dst[:, :], None, slice(c0, c0 + P), uh[:, k, :], ul[:, k, :], k == 0, k == LB - 1)
            elif name == "a":
                if i == 0:
                    for k in range(2):
                        ck.wait(t_pool, r, "gh", k)
                        ck.wait(t_dve, r, "gl", k)
                e, n = SEQ[i]
                for k in range(2):
                    c0 = C_W1 + (FIRST[e] + n) * LAT + k * P
                    m = three(dst[:, :], None, slice(c0, c0 + P), gh[:, k, :], gl[:, k, :], k == 0, k == 1)
            elif name == "gt":
                ck.wait(t_dve, r, "r", "G")
                for t in range(G4):
                    m = pe.transpose(dst[:, t * P:t * P + P], Gp[:, t, :], ident)
            elif name == "y":
                e, n = SEQ[i]
                o = ORDER.index(e)
                if i == 0 and r == 0:
                    pe.wait_ge(t_z.sem, 7)
                if n == 0:
                    if o >= 2:
                        ck.wait(t_dve, r, "acc", ORDER[o - 2], G4 - 1)
                    else:
                        ck.wait(t_dve, r - 1, "acc", ORDER[-1], G4 - 1)
                ck.wait(t_pool, r, "ah", i)
                ck.wait(t_dve, r, "al", i)
                for t in range(G4):
                    first = n == 0 and t % 2 == 0
                    dst = Y[o % 2][:, t, :]
                    if e == E and n == 0:
                        if t == 0:
                            ck.wait(t_act, r, "gt", 0)
                        pe.matmul(dst, GT[:, t * P:t * P + P], Z[:, :], start=first, stop=False, skip_group_check=True)
                        first = False
                    c0 = C_W2 + (FIRST[e] + n) * LAT
                    cols = slice(t * P, t * P + P)
                    m = three(dst, None, slice(c0, c0 + LAT), ah[i % 3][:, cols], al[i % 3][:, cols], first,
                              n == TILES[e] - 1, swap=True, skip=True)
            elif name == "core":
                for k in range(LB):
                    if i == 0:
                        ck.wait(t_pool, r, "guh", k)
                        ck.wait(t_dve, r, "gul", k)
                    c0, cols = C_CORE + k * L, slice(i * P, i * P + P)
                    m = three(dst[:, :], None, slice(c0, c0 + L), guh[:, k, cols], gul[:, k, cols], k == 0, False, swap=True)
            elif name == "ot":
                for t in range(G4):
                    if i == 0:
                        ck.wait(t_dve, r, "acc", ORDER[-1], t)
                    m = pe.transpose(dst[:, t * P:t * P + P], acc[:, t, i * P:i * P + P], ident)
            elif name == "fin":
                for k in range(2):
                    if i == 0:
                        ck.wait(t_dve, r, "ot", k)
                    c0, cols = C_UP + k * L, slice(i * P, i * P + P)
                    m = three(dst[:, :], None, slice(c0, c0 + L), oh[:, k, cols], ol[:, k, cols], False, k == 1, swap=True)
            m.then_inc(t_pe.sem, 1)

        over_groups(pe, pe_ops, do)

    @block.scalar
    def _(act):
        act.wait_ge(t_in.sem, 16 * 6)
        act.activation(gb[:, :], bc[:, 0:NT], ACT.Gelu).then_inc(t_z.sem, 1)
        act.wait_ge(t_z.sem, 4)
        act.copy(zs[:, :], Y[0][:, 0, :]).then_inc(t_z.sem, 1)
        act.wait_ge(t_z.sem, 6)
        act.copy(Z[:, :], Y[1][:, 0, :]).then_inc(t_z.sem, 1)

        def do(ck, r, name, i):
            if name in ("uT", "lg", "h", "a", "gt", "ot"):
                src = H[bank[(name, i)]][:, :]
                ck.wait(t_pe, r, name, i)
            if name == "uT":
                ck.wait(t_pool, r - 1, "guh", i)
                ck.wait(t_dve, r - 1, "gul", i)
                m = act.copy(uf[:, i, :], src)
            elif name == "lg":
                m = act.copy(lp[:, :], src)
            elif name == "h":
                m = act.activation(gf_[:, i, :], src, ACT.Gelu, bias=bc[:, NTS + i:NTS + i + 1])
            elif name == "a":
                e, n = SEQ[i]
                ck.wait(t_pool, *((r, "ah", i - 3) if i >= 3 else (r - 1, "ah", i - 3 + NA)))
                ck.wait(t_dve, *((r, "al", i - 3) if i >= 3 else (r - 1, "al", i - 3 + NA)))
                b_ = FIRST[e] + n
                m = act.activation(af[i % 3][:, :], src, ACT.Gelu, bias=bc[:, b_:b_ + 1])
            elif name == "gu":
                ck.wait(t_pool, r, "uh", i)
                ck.wait(t_dve, r, "ul", i)
                ck.wait(t_pe, r, "lg", 0)
                m = act.activation(uf[:, i, :], uf[:, i, :], ACT.Gelu)
            elif name == "gt":
                m = act.copy(GT[:, :], src)
            elif name == "ot":
                ck.wait(t_pe, r - 1, "fin", G4 - 1)
                m = act.copy(oh[:, i, :], src)
            m.then_inc(t_act.sem, 1)

        over_groups(act, act_ops, do)

    @block.vector
    def _(dve):
        dve.memset(Gp[:, :, :], 0.0).then_inc(t_zd.sem, 1)
        dve.memset(gbh[:, :, :], 0.0).then_inc(t_zd.sem, 1)
        dve.memset(gbl[:, :, :], 0.0).then_inc(t_zd.sem, 1)
        dve.wait_ge(t_zd.sem, 3)
        dve.memset(Gp[:, :, E:E + 1], 1.0).then_inc(t_zd.sem, 1)
        dve.wait_ge(t_z.sem, 1)
        for e in range(E):
            n = slice(FIRST[e], FIRST[e] + TILES[e])
            m = dve.tensor_copy(gbh[:, n, e], gb[:, n])
        m.then_inc(t_z.sem, 1)
        dve.wait_ge(t_z.sem, 2)
        for e in range(E):
            n = slice(FIRST[e], FIRST[e] + TILES[e])
            m = dve.tensor_tensor(gbl[:, n, e], gb[:, n], gbh[:, n, e], ALU.subtract)
        m.then_inc(t_z.sem, 1)
        dve.wait_ge(t_in.sem, 16 * 6)
        dve.tensor_tensor(rbb[:, :, :], rbb[:, :, :], cst[:, K_COST:K_COST + G4 * E].rearrange("p (t e) -> p t e", t=G4),
                          ALU.subtract).then_inc(t_zd.sem, 1)
        dve.wait_ge(t_zd.sem, 5)
        wide = lambda v: v.unsqueeze(2).broadcast_to([P, G4, E])
        R = lambda n: red[:, n, :]
        iota = cst[:, K_IOTA:K_IOTA + E].unsqueeze(1).broadcast_to([P, G4, E])

        def route(ck, r, what):
            own = lambda n, apart=False: ck.wait(t_dve, r, "r", n, apart=apart)
            if what == "lred":
                ck.wait(t_pe, r, "lt", 0)
                src = H[bank[("lt", 0)]][:, :].rearrange("p (t k c) -> p t c k", t=G4, k=LB)
                return dve.tensor_reduce(lg[:, :, :], src[:, :, 0:E, :], AX.X, ALU.add)
            if what == "lb":
                own("lred")
                return dve.tensor_tensor(lg[:, :, :], lg[:, :, :], rbb[:, :, :], ALU.add)
            if what == "lmx":
                own("lb")
                return dve.tensor_reduce(R(0), lg[:, :, :], AX.X, ALU.max)
            if what == "lsub":
                own("lmx")
                return dve.tensor_tensor(lg[:, :, :], lg[:, :, :], wide(R(0)), ALU.subtract)
            if what == "psum":
                ck.wait(t_pool, r, "pexp", 0)
                return dve.tensor_reduce(R(1), pe_[:, :, :], AX.X, ALU.add)
            if what == "prcp":
                own("psum")
                return dve.reciprocal(R(2), R(1))
            if what == "pp":
                own("prcp")
                return dve.tensor_tensor(pp[:, :, :], pe_[:, :, :], wide(R(2)), ALU.mult)
            if what[:3] == "max":
                own("pp", apart=True)
                t = int(what[3:])
                return dve.max(t8[:, t, :], pp[:, t, :])
            if what[:3] == "idx":
                own("max" + what[3:], apart=True)
                t = int(what[3:])
                return dve.max_index(t8i[:, t, :], t8[:, t, :], pp[:, t, :])
            if what == "tif":
                own("idx3")
                return dve.tensor_copy(tif[:, :, :], t8i[:, :, 0:2])
            if what == "dz":
                return dve.tensor_tensor(R(3), t8[:, :, 1], t8[:, :, 0], ALU.subtract)
            if what == "e1":
                ck.wait(t_pool, r, "e2", 0)
                return dve.tensor_scalar(R(5), R(4), 1.0, None, ALU.add)
            if what == "g1":
                own("e1")
                return dve.reciprocal(R(6), R(5))
            if what == "g2":
                own("g1")
                return dve.tensor_tensor(R(7), R(4), R(6), ALU.mult)
            if what in ("m1", "m2"):
                own("tif")
                n = int(what[1]) - 1
                return dve.tensor_tensor((m1, m2)[n][:, :, :], iota, wide(tif[:, :, n]), ALU.is_equal)
            if what in ("G1", "G2"):
                n = int(what[1]) - 1
                own("m1" if n == 0 else "m2")
                own("g2")
                m = (m1, m2)[n][:, :, :]
                return dve.tensor_tensor(m, m, wide(R(6 + n)), ALU.mult)
            own("G2")
            ck.wait(t_pe, r - 1, "gt", 0)
            return dve.tensor_tensor(Gp[:, :, 0:E], m1[:, :, :], m2[:, :, :], ALU.add)

        def do(ck, r, name, i, t=None):
            if name == "ul":
                ck.wait(t_act, r, "uT", i)
                ck.wait(t_pool, r, "uh", i)
                ck.wait(t_pe, r - 1, "h", 1)
                m = dve.tensor_tensor(ul[:, i, :], uf[:, i, :], uh[:, i, :], ALU.subtract)
            elif name == "gl":
                ck.wait(t_pool, r, "gh", i)
                m = dve.tensor_tensor(gl[:, i, :], gf_[:, i, :], gh[:, i, :], ALU.subtract)
            elif name == "gul":
                ck.wait(t_pool, r, "guh", i)
                m = dve.tensor_tensor(gul[:, i, :], uf[:, i, :], guh[:, i, :], ALU.subtract)
            elif name == "al":
                ck.wait(t_pool, r, "ah", i)
                if SEQ[i][0] == E:
                    m = dve.scalar_tensor_tensor(out=al[i % 3][:, :], in0=af[i % 3][:, :], scalar=0.1, in1=ah[i % 3][:, :],
                                                 op0=ALU.mult, op1=ALU.subtract)
                else:
                    m = dve.tensor_tensor(al[i % 3][:, :], af[i % 3][:, :], ah[i % 3][:, :], ALU.subtract)
            elif name == "acc":
                e = i
                o = ORDER.index(e)
                if t == 0:
                    ck.wait(t_pe, r, "y", y_last(e))
                y = Y[o % 2][:, t, :]
                a = acc[:, t, :]
                if o == 0:
                    ck.wait(t_pe, r - 1, "ot", 1)
                    ck.wait(t_dve, r, "r", "G")
                    m = dve.tensor_scalar(a, y, Gp[:, t, e:e + 1], None, ALU.mult)
                else:
                    ck.wait(t_dve, r, "acc", ORDER[o - 1], t)
                    if e == E:
                        m = dve.tensor_tensor(a, y, a, ALU.add)
                    else:
                        m = dve.scalar_tensor_tensor(out=a, in0=y, scalar=Gp[:, t, e:e + 1], in1=a, op0=ALU.mult, op1=ALU.add)
            elif name == "stats":
                ck.wait(t_pool, r, "x1", i)
                m = dve.bn_stats(st[:, i, :], X[:, i, :])
            elif name == "aggr":
                ck.wait(t_dve, r, "stats", i, apart=True)
                m = dve.bn_aggr(mv[:, i, :], st[:, i, :])
            elif name == "ot":
                ck.wait(t_act, r, "ot", i)
                m = dve.tensor_tensor(ol[:, i, :], H[bank[("ot", i)]][:, :], oh[:, i, :], ALU.subtract)
            elif name == "fin":
                ck.wait(t_pe, r, "fin", i)
                ck.wait(t_pool, r, "xb", i)
                m = dve.scalar_tensor_tensor(out=XB[:, i, :], in0=H[bank[("fin", i)]][:, :], scalar=gate[:, 4:5],
                                             in1=XB[:, i, :], op0=ALU.mult, op1=ALU.add)
            elif name == "r":
                m = route(ck, r, i)
            m.then_inc(t_dve.sem, 1)

        over_groups(dve, dve_ops, do)

    @block.gpsimd
    def _(pool):
        pool.wait_ge(t_in.sem, 16 * 6)
        pool.tensor_tensor(tb[:, :], tb[:, :], tb2[:, :], ALU.add).then_inc(t_zp.sem, 1)
        pool.wait_ge(t_zp.sem, 1)
        pool.tensor_scalar(tb[:, :], tb[:, :], gate[:, 4:5], 1.0, ALU.mult, ALU.mult).then_inc(t_zp.sem, 1)
        pool.wait_ge(t_zp.sem, 2)
        cast = lambda dst, src, by=1.0: pool.tensor_scalar(dst, src, by, 1.0, ALU.mult, ALU.mult)
        base = cst[:, K_E:K_E + G4 * E]

        def do(ck, r, name, i):
            if name == "uh":
                ck.wait(t_act, r, "uT", i)
                ck.wait(t_pe, r - 1, "h", 1)
                m = cast(uh[:, i, :], uf[:, i, :])
            elif name == "gh":
                ck.wait(t_act, r, "h", i)
                ck.wait(t_pe, r - 1, "a", NA - 1)
                m = cast(gh[:, i, :], gf_[:, i, :])
            elif name == "guh":
                ck.wait(t_act, r, "gu", i)
                ck.wait(t_pe, r - 1, "fin", G4 - 1)
                m = cast(guh[:, i, :], uf[:, i, :])
            elif name == "ah":
                ck.wait(t_act, r, "a", i)
                ck.wait(t_pe, *((r, "y", i - 3) if i >= 3 else (r - 1, "y", i - 3 + NA)))
                m = cast(ah[i % 3][:, :], af[i % 3][:, :], 0.1 if SEQ[i][0] == E else 1.0)
            elif name == "pexp":
                ck.wait(t_dve, r, "r", "lsub")
                m = pool.tensor_tensor(pe_[:, :, :].rearrange("p t e -> p (t e)"), base, lg[:, :, :].rearrange("p t e -> p (t e)"), ALU.pow)
            elif name == "e2":
                ck.wait(t_dve, r, "r", "dz")
                m = pool.tensor_tensor(red[:, 4, :], base[:, 0:G4], red[:, 3, :], ALU.pow)
            elif name == "xb":
                ck.wait(t_o, r - 1)
                m = pool.tensor_tensor(XB[:, i, :], X[:, i, :], tb[:, :], ALU.add)
            elif name == "x1":
                ck.wait(t_xx, r)
                m = pool.tensor_tensor(X[:, i, :], X[:, i, :], XA[:, i, :], ALU.add)
            elif name == "negm":
                ck.wait(t_dve, r, "aggr", G4 - 1)
                m = pool.tensor_scalar(lnv[:, 0, :], mv[:, :, 0], -1.0, 1.0, ALU.mult, ALU.mult)
            elif name == "rstd" and i == 0:
                m = pool.tensor_scalar(lnv[:, 1, :], mv[:, :, 1], EPS, None, ALU.add)
            elif name == "rstd":
                ck.wait(t_pool, r, "rstd", 0)
                m = pool.tensor_tensor(lnv[:, 1, :], lnv[:, 1, :], cst[:, K_PH:K_PH + 1].broadcast_to([P, G4]), ALU.pow)
            elif name == "u":
                ck.wait(t_pool, r, "rstd", 1)
                ck.wait(t_pe, r - 1, "uT", LB - 1)
                m = pool.tensor_scalar(u[:, i, :], X[:, i, :], lnv[:, 0, i:i + 1], lnv[:, 1, i:i + 1], ALU.add, ALU.mult)
            m.then_inc(t_pool.sem, 1)

        over_groups(pool, pool_ops, do, apart=True)


def kernel(**inputs):
    import concourse.bacc as bacc
    from concourse.bass_utils import run_bass_kernel_spmd

    nc = bacc.Bacc("TRN2", target_bir_lowering=False, num_devices=1)
    wall, bcol, b2, rw = pack(inputs)
    g = lambda n: np.ascontiguousarray(inputs[n])
    data = {
        "x": g("x"), "ctx_kv": g("ctx_2048"), "gx": g("g_xattn"), "gf": g("g_ffn"),
        "gamma": g("L0_xattn_gamma").reshape(1), "wall": wall, "bcol": bcol, "b2": b2, "rw": rw,
        "rb": g("L0_ffn_router_b"), "upb": g("L0_ffn_up_b"), "coreb": g("L0_ffn_core_b"),
        "const": constants(), "ones": np.ones((1, 2 * QUADS * L), np.float16),
    }
    args = {n: nc.dram_tensor(f"in_{n}", a.shape, mybir.dt.from_np(a.dtype), kind="ExternalInput").ap()
            for n, a in data.items()}
    out = nc.dram_tensor("out_0", (B, D, L), F32, kind="ExternalOutput").ap()
    program(nc, *args.values(), out)
    r = run_bass_kernel_spmd(nc, [{f"in_{n}": a for n, a in data.items()}], core_ids=[0])
    return r.results[0]["out_0"]
```

```python
from contextlib import ExitStack

import numpy as np

import concourse.bass as bass
from concourse import mybir

F32 = mybir.dt.float32
F16 = mybir.dt.float16
U32 = mybir.dt.uint32
ALU = mybir.AluOpType
ACT = mybir.ActivationFunctionType
AX = mybir.AxisListType

P = 128
B, D, L = 16, 128, 512
NH, DH = 8, 16
QUADS = NH // 2
LB = L // P
SCALE = DH ** -0.5
EPS = 1e-5
HID = [256, 512, 768, 1024, 256, 512, 768, 1024]
E = len(HID)
LAT = 256
NT = sum(HID) // P
COST_LAMBDA = 1e-7
TILES = [h // P for h in HID] + [LAT // P]
FIRST = [sum(TILES[:e]) for e in range(E + 1)]
NTS = sum(TILES)
C_W1 = 0
C_W2 = C_W1 + NTS * LAT
C_DOWN = C_W2 + NTS * LAT
C_CORE = C_DOWN + LB * LAT
C_UP = C_CORE + LB * L
NCOL = C_UP + 2 * L
WCH = NCOL // B
R_ZERO = 127
R_MAX = 127
K_ID, K_M1, K_M2, K_ME, K_MO, K_PH, K_IOTA, K_COST, K_E = 0, 128, 256, 384, 385, 386, 388, 396, 428
NCONST = 460


class Tally:

    def __init__(self, sem, step=1):
        self.sem, self.step, self.value, self.at = sem, step, 0, {}

    def plan(self, *key, n=1):
        self.value += self.step * n
        self.at[key] = self.value


class Clock:

    def __init__(self, eng, period, setup, apart=False):
        self.eng, self.turn, self.period, self.setup = eng, None, period, setup
        self.apart = apart

    def wait(self, tally, *key, apart=False):
        if key not in tally.at:
            assert self.turn is None and key[0] < 0
            return
        v = tally.at[key]
        if self.turn is not None:
            later = (key[0] + self.period,) + key[1:]
            v = v + self.turn * (tally.at[later] - v)
            if apart or self.apart:
                v = self.eng.to_reg(v)
                self.eng.wait_ge(self.setup.sem, self.setup.value)
        self.eng.wait_ge(tally.sem, v)

    def index(self, n):
        return n if self.turn is None else n + self.turn * self.period


def pack(inputs):
    f = lambda a: np.asarray(a)
    kt = lambda w: f(w).reshape(-1, P, f(w).shape[1]).transpose(1, 0, 2)
    g = lambda n: inputs["L0_ffn_" + n]
    experts = [f"e{e}_" for e in range(E)] + ["shared_"]
    w1 = [kt(g(n + "w1")).reshape(P, 2, -1, P).transpose(0, 2, 1, 3).reshape(P, -1) for n in experts]
    w2 = [kt(g(n + "w2")).reshape(P, -1) for n in experts]
    rest = [kt(g(n)).reshape(P, -1) for n in ("down_w", "core_w", "up_w")]
    wall = np.ascontiguousarray(np.concatenate(w1 + w2 + rest, 1))
    col = lambda n: f(g(n)).reshape(-1, P).T
    bcol = np.ascontiguousarray(np.concatenate(
        [col(n + "b1") for n in experts] + [col("down_b")], 1))
    b2 = np.zeros((P, LAT), np.float32)
    for e in range(E):
        b2[e] = f(g(f"e{e}_b2"))
    b2[E] = f(g("shared_b2"))
    rw = np.zeros((P, LB, 32), np.float32)
    rw[:, :, :E] = kt(g("router_w"))
    return wall, bcol, b2, rw


def constants():
    c = np.zeros((P, NCONST), np.float32)
    c[:, K_ID:K_ID + P] = np.eye(P)
    for q in range(4):
        c[32 * q:32 * q + E, K_M1:K_M1 + E] = 1 - np.eye(E)
    c[0:E, K_M2:K_M2 + E] = 1
    c[E, K_M2 + E] = 0.1
    even = (np.arange(P) % 32) < DH
    c[:, K_ME], c[:, K_MO] = even, ~even
    c[:, K_PH] = -0.5
    c[:, K_IOTA:K_IOTA + E] = np.arange(E)
    c[:, K_COST:K_COST + 4 * E] = np.tile(np.float32(COST_LAMBDA) * np.array([2 * LAT * h for h in HID], np.float32), 4)
    c[:, K_E:K_E + 4 * E] = np.e
    return c


def program(nc, x, ctx_kv, gx, gf, gamma, wall, bcol, b2, rw, rb, upb, coreb, const, ones, out):
    att = nc.dram_tensor("att_scratch", [B, P, L], F32, kind="Internal").ap()
    sq = nc.dram_tensor("q_scratch", [B, 2, P, L], F16, kind="Internal").ap()
    sk = nc.dram_tensor("k_scratch", [B, 2, P, L], F16, kind="Internal").ap()
    sd = nc.dram_tensor("den_scratch", [B, 2, NH, L], F32, kind="Internal").ap()
    with ExitStack() as whole:
        ps = lambda n, s, c: c.enter_context(nc.psum_tensor(n, s, F32))
        sb = lambda n, s, d=F32, c=whole: c.enter_context(nc.sbuf_tensor(n, s, d))
        sem = lambda n: whole.enter_context(nc.semaphore(n))
        keep = {
            "cst": sb("cst", [P, NCONST]), "whi": sb("whi", [P, NCOL], F16), "wlo": sb("wlo", [P, NCOL], F16),
            "gate": sb("gate", [P, 6]),
            "X": sb("X", [P, G4, L]), "XA": sb("XA", [P, G4, L]), "u": sb("u", [P, G4, L]),
        }
        with ExitStack() as c:
            parts_a, ends = attention(nc, c, keep, sb, ps, sem, x, ctx_kv, gx, gf, gamma, wall, const, ones, att, sq, sk, sd)
        with ExitStack() as c:
            parts_b = ffn(nc, c, keep, sb, ps, sem, ends, x, att, bcol, b2, rw, rb, upb, coreb, out)
            block = c.enter_context(nc.Block())

            def both(name):
                def run(eng):
                    tail, rest = parts_b[name](eng)
                    parts_a[name](eng, tail)
                    rest()
                return run

            block.sync(both("sync"))
            block.tensor(both("tensor"))
            block.scalar(both("scalar"))
            block.vector(both("vector"))
            block.gpsimd(both("gpsimd"))


def attention(nc, c, keep, sb, ps, sem, x, ctx_kv, gx, gf, gamma, wall, const, ones, att, sq, sk, sd):
    cst, whi, wlo, gate = keep["cst"], keep["whi"], keep["wlo"], keep["gate"]
    ident = cst[:, K_ID:K_ID + P]
    A = lambda n, s, d=F32: sb(n, s, d, c)
    X, XA, u = keep["X"], keep["XA"], keep["u"]
    xt = [X[:, i, :] for i in range(2)]
    ct = [X[:, 2 + i, :] for i in range(2)]
    wst = [v[:, :, :].rearrange("p t q -> p (t q)")[:, 0:WCH] for v in (XA, u)]
    stacks = lambda i: [A(f"{n}{i}", [P, 2, QUADS, L], F16) for n in ("QS", "KS")] + [A(f"VT{i}", [P, LB, 2, QUADS, 32])]
    pair = [stacks(0)]
    qhl = [A(f"qhl{i}", [P, 2, L], F16) for i in range(2)]
    khl = [A(f"khl{i}", [P, 2, L], F16) for i in range(2)]
    qf, stats = A("qf", [P, L]), A("stats", [P, 6])
    pair.append(stacks(1))
    QS, KS, VT = zip(*pair)
    mx = A("mx", [P, 32])
    mrow = A("mrow", [16, P], F16)
    Pb = [A(f"P{i}", [P, L]) for i in range(8)]
    mv = [A(f"mv{i}", [P, 2]) for i in range(2)]
    ln = [A(f"ln{i}", [P, 4]) for i in range(2)]
    U = [A(f"U{g}", [P, L]) for g in range(2)]
    tn = A("tn", [P, L])
    cme = A("cme", [P, 2])
    dc, rc = A("dc", [P, NH * L // P]), A("rc", [P, NH * L // P])
    rd = A("rd", [P, L])
    ao = [A(f"ao{i}", [P, L]) for i in range(2)]
    nat = [ps(f"nat{i}", [P, 2, L], c) for i in range(2)]
    ring = [ps(f"ring{i}", [P, L], c) for i in range(3)]
    pv = ps("pv", [P, L], c)

    T = lambda n, step=1: Tally(sem(n), step)
    t_cst, t_gates, t_one, t_vt, t_gate = T("a_cst", 16), T("a_gates", 16), T("a_ones", 16), T("a_vt"), T("a_gate")
    t_set = [T(f"a_set{i}") for i in range(2)]
    t_x, t_c, t_wl = ([T(f"{n}_in{i}", 16) for i in range(2)] for n in ("x", "ctx", "w"))
    t_sq, t_sk = T("q_out", 16), T("k_out", 16)
    t_stk = [T(f"stack_in{g}", 16) for g in range(2)]
    t_m = [T(f"max_row_in{g}", 16) for g in range(2)]
    t_ds, t_dc, t_rs, t_rb = T("den_out", 16), T("den_in", 16), T("recip_out", 16), T("recip_in", 16)
    t_st = T("att_out", 16)
    t_nat, t_ring, t_pv = T("pe_nat"), T("pe_ring"), T("pe_pv")
    t_use, t_ev = T("act_ring"), T("act_evac")
    t_wh = T("act_whi")
    t_max, t_dve, t_pool = T("dve_max"), T("dve_small"), T("pool")

    t_cst.plan("all")
    STEPS, BEHIND = 8, 8

    def pe_jobs(w):
        jobs = []
        for s in range(STEPS):
            t, n = divmod(STEPS * w + s - BEHIND, STEPS)
            for half in range(2):
                if w < B:
                    jobs.append(("nat", w, 2 * s + half))
                if 0 <= t < B:
                    jobs += [("st", t, n, 2 * half), ("st", t, n, 2 * half + 1)]
            t, n = divmod(STEPS * w + s - BEHIND - 1, STEPS)
            if 0 <= t < B:
                jobs.append(("pv", t, n))
            if s == 0 and 1 <= w <= B:
                jobs.append(("m", w - 1, 1))
            if s == 1 and w < B:
                jobs += [("vt", w, 0), ("vt", w, 1)]
            if s == 5 and w < B:
                jobs.append(("m", w, 0))
        return jobs

    WINDOWS = range(B + 2)
    ring_keys = []
    for w in WINDOWS:
        for kind, *key in pe_jobs(w):
            if kind == "nat":
                t_nat.plan(*key); t_max.plan(*key)
            elif kind == "pv":
                t_pv.plan(*key)
                if key[1] % 4 == 3:
                    t_ev.plan(key[0], key[1] // 4)
            else:
                k = (key[0], kind, *key[1:])
                ring_keys.append(k)
                t_ring.plan(*k); t_use.plan(*k)
    place = {k: n for n, k in enumerate(ring_keys)}

    def dve_small(w):
        return ([(w + 1, "stats"), (w + 1, "aggr")] if w + 1 < B else []) + \
               ([(w - 2, "recip")] if w >= 2 else [])

    def pool_jobs(w):
        jobs = []
        if w + 1 < B:
            keys, queries = ("kh", "kl"), ("negm", "veps", "rstd", "rs", "qf", "qh", "ql")
            jobs += [(w + 1, n) for n in (queries + keys if w < 0 else keys + queries)]
        if w >= 2:
            jobs += [(w - 2, n) for n in ("na", "nb", "num")]
        if 0 <= w < B:
            jobs += [(w, "wlo")]
        if w >= 2:
            jobs += [(w - 2, "att")]
        return jobs

    for w in range(-1, B + 2):
        for k in dve_small(w):
            t_dve.plan(*k)
        for k in pool_jobs(w):
            t_pool.plan(*k)
        if w + 1 < B:
            for t_ in (t_x[(w + 1) % 2], t_c[(w + 1) % 2], t_sq, t_sk):
                t_.plan(w + 1)
            for g in range(2):
                t_stk[g].plan(w + 1, n=6)
        if 0 <= w < B:
            t_wl[w % 2].plan(w)
            t_wh.plan(w)
            for g in range(2):
                t_m[g].plan(w)
        if w >= 2:
            t_ds.plan(w - 2, n=2)
            t_rb.plan(w - 2)
            for t_ in (t_dc, t_rs, t_st):
                t_.plan(w - 2)

    def over_windows(eng, body, tail, apart=False):
        ck = Clock(eng, 2, t_cst, apart)
        for w in range(-1, 4):
            body(ck, w)
        with eng.Fori(0, (B - 6) // 2) as turn:
            ck.turn = turn
            body(ck, 4)
            body(ck, 5)
        ck.turn = None
        for w in range(B - 2, B + 2):
            tail.get(w, lambda: None)()
            body(ck, w)

    def sync(sp, tail):
        def stack(ck, b, g, side):
            scr, dst, parts, stored = ((sq, QS[b % 2], (0, 1, 0), t_sq), (sk, KS[b % 2], (0, 0, 1), t_sk))[side]
            ck.wait(stored, b)
            ck.wait(t_ring, b - 2, "st", 4 * g + 3, 3)
            if b < 2:
                sp.wait_ge(t_set[b].sem, 2)
            for n, part in enumerate(parts):
                src = scr[ck.index(b), part].rearrange("(j g d) q -> g d j q", g=2, d=DH)[g]
                sp.dma_start(dst[DH * n:DH * n + DH, g, :, :], src).then_inc(t_stk[g].sem, 16)

        def row_of_ones(i):
            sp.wait_ge(t_set[i].sem, 2)
            sp.dma_start(KS[i][R_MAX:R_MAX + 1, :, :, :].rearrange("o g j q -> o (g j q)"), ones).then_inc(t_one.sem, 16)

        def load_x(ck, b):
            ck.wait(t_pool, b - 2, "qf")
            sp.dma_start(xt[b % 2], x[ck.index(b)]).then_inc(t_x[b % 2].sem, 16)

        def load_ctx(ck, b):
            ck.wait(t_pool, b - 2, "kl")
            ck.wait(t_ring, b - 2, "vt", 1)
            sp.dma_start(ct[b % 2], ctx_kv[ck.index(b)]).then_inc(t_c[b % 2].sem, 16)

        def load_weights(ck, n):
            ck.wait(t_pool, n - 2, "wlo")
            sp.dma_start(wst[n % 2], wall[:, bass.ds(ck.index(n) * WCH, WCH)]).then_inc(t_wl[n % 2].sem, 16)

        def body(ck, w):
            b, t = w + 1, w - 2
            if w < 0:
                load_x(ck, 0)
                sp.dma_start(cst[:, :], const).then_inc(t_cst.sem, 16)
                load_ctx(ck, 0)
                for dst, src in ((gate[:, 0:1], gx.partition_broadcast(P)),
                                 (gate[:, 1:2], gf.partition_broadcast(P)), (gate[:, 2:3], gamma.partition_broadcast(P))):
                    sp.dma_start(dst, src).then_inc(t_gates.sem, 16)
                load_x(ck, 1)
                load_ctx(ck, 1)
                load_weights(ck, 0)
            if 0 <= w < B - 2:
                load_x(ck, w + 2)
            if 0 <= w < B - 1:
                load_weights(ck, w + 1)
            if t >= 0:
                ck.wait(t_ev, t, 1)
                for g in range(2):
                    r = DH * (1 - g)
                    sp.dma_start(sd[ck.index(t), 0].rearrange("(j g) q -> g j q", g=2)[g], U[g][r:P:32, :]).then_inc(t_ds.sem, 16)
            if 0 <= w < B - 2:
                load_ctx(ck, w + 2)
            if t >= 0:
                ck.wait(t_ds, t)
                ck.wait(t_dve, t - 1, "recip")
                sp.dma_start(dc[:, :], sd[ck.index(t), 0].rearrange("h (s q) -> (h s) q", s=P // NH)).then_inc(t_dc.sem, 16)
            if b < B:
                for side in ((0, 1) if w < 0 else (1, 0)):
                    scr, parts, t_, last = ((sq, qhl, t_sq, "ql"), (sk, khl, t_sk, "kl"))[side]
                    ck.wait(t_pool, b, last)
                    sp.dma_start(scr[ck.index(b)].rearrange("t p q -> p t q"), parts[b % 2][:, :, :]).then_inc(t_.sem, 16)
                stack(ck, b, 0, 0 if w < 0 else 1)
                stack(ck, b, 0, 1 if w < 0 else 0)
            tail.get((w, "loads"), lambda: None)()
            if t >= 0:
                ck.wait(t_dve, t, "recip")
                sp.dma_start(sd[ck.index(t), 1].rearrange("h (s q) -> (h s) q", s=P // NH), rc[:, :]).then_inc(t_rs.sem, 16)
                ck.wait(t_rs, t)
                ck.wait(t_pool, t - 1, "att")
                sp.dma_start(rd[:, :], sd[ck.index(t), 1].unsqueeze(1).broadcast_to([NH, DH, L])).then_inc(t_rb.sem, 16)
                ck.wait(t_pool, t, "att")
                sp.dma_start(att[ck.index(t)], ao[t % 2][:, :]).then_inc(t_st.sem, 16)
            if b < B:
                stack(ck, b, 1, 1)
                stack(ck, b, 1, 0)
            if w < 0:
                row_of_ones(0)
                row_of_ones(1)

        over_windows(sp, body, tail, apart=True)

    def tensor(pe, tail):
        pe.wait_ge(t_cst.sem, 16)

        def ring_free(ck, key):
            n = place[key] - 3
            if n >= 0:
                ck.wait(t_use, *ring_keys[n])

        def body(ck, w):
            if w < 0:
                return
            for kind, b, *rest in pe_jobs(w):
                i = b % 2
                if kind == "nat":
                    k, = rest
                    g, j = k // 8, k % 8 // 2
                    if k % 8 == 0:
                        ck.wait(t_stk[g], b)
                    ck.wait(t_max, *((b, k - 2) if k >= 2 else (b - 1, k + 14)))
                    for h in range(2):
                        q0 = (2 * (k % 2) + h) * P
                        m = pe.matmul(nat[k % 2][:, h, :], QS[i][0:R_ZERO, g, j, q0:q0 + P], KS[i][0:R_ZERO, g, j, :],
                                      start=True, stop=True)
                    m.then_inc(t_nat.sem, 1)
                elif kind == "st":
                    s, j = rest
                    g, lb = s // 4, s % 4
                    if lb == 0 and j == 0:
                        ck.wait(t_m[g], b)
                        if b == 0 and g == 0:
                            pe.wait_ge(t_one.sem, 16 * 2)
                    key = (b, "st", s, j)
                    ring_free(ck, key)
                    pe.matmul(ring[place[key] % 3][:, :], KS[i][0:R_MAX + 1, g, j, lb * P:lb * P + P],
                              QS[i][0:R_MAX + 1, g, j, :], start=True, stop=True).then_inc(t_ring.sem, 1)
                elif kind == "pv":
                    s, = rest
                    g, lb = s // 4, s % 4
                    if s == 0:
                        ck.wait(t_use, b, "vt", 1)
                    if lb == 0:
                        ck.wait(t_ev, *((b, 0) if g else (b - 1, 1)))
                    ck.wait(t_use, b, "st", s, 3)
                    for j in range(QUADS):
                        m = pe.matmul(pv[32 * j:32 * j + 32, :], VT[i][:, lb, g, j, :], Pb[4 * (s % 2) + j][:, :],
                                      start=(lb == 0), stop=(lb == 3))
                    m.then_inc(t_pv.sem, 1)
                elif kind == "m":
                    g, = rest
                    key = (b, "m", g)
                    ck.wait(t_max, b, 8 * g + 7)
                    ring_free(ck, key)
                    pe.transpose(ring[place[key] % 3][0:16, 0:P], mx[:, 16 * g:16 * g + 16], ident).then_inc(t_ring.sem, 1)
                else:
                    a, = rest
                    key = (b, "vt", a)
                    if a == 0:
                        ck.wait(t_c[b % 2], b)
                    ring_free(ck, key)
                    for n in range(2):
                        lb = 2 * a + n
                        m = pe.transpose(ring[place[key] % 3][:, n * P:n * P + P], ct[i][:, lb * P:lb * P + P], ident)
                    m.then_inc(t_ring.sem, 1)

        over_windows(pe, body, tail)

    def scalar(act, tail):
        act.wait_ge(t_gates.sem, 16 * 3)
        act.activation(gate[:, 3:5], gate[:, 0:2], ACT.Tanh).then_inc(t_gate.sem, 1)
        act.wait_ge(t_vt.sem, 2)

        def max_row(ck, b, g):
            ck.wait(t_use, b, "m", g)
            act.dma_start(QS[b % 2][R_MAX:R_MAX + 1, g, :, :].rearrange("o j q -> o (j q)").rearrange("o (r p) -> o r p", p=P),
                          mrow[:, :]).then_inc(t_m[g].sem, 16)

        def body(ck, w):
            if w < 0:
                return
            row = None
            for kind, b, *rest in pe_jobs(w):
                i = b % 2
                if kind == "nat":
                    n, piece = rest[0] // 2 - 3, WCH // 4
                    if rest[0] % 2 == 0 and 0 <= n < 4:
                        if n == 0:
                            ck.wait(t_wl[w % 2], w)
                        m = act.copy(whi[:, bass.ds(ck.index(w) * WCH + n * piece, piece)], wst[w % 2][:, n * piece:(n + 1) * piece])
                        if n == 3:
                            m.then_inc(t_wh.sem, 1)
                    continue
                if kind == "pv":
                    s, = rest
                    if s % 4 == 3:
                        g = s // 4
                        ck.wait(t_pv, b, s)
                        ck.wait(t_pool, b - 1, "nb")
                        ck.wait(t_ds, b - 1)
                        act.copy(U[g][:, :], pv[:, :]).then_inc(t_ev.sem, 1)
                    continue
                key = (b, kind, *rest)
                bank = ring[place[key] % 3]
                ck.wait(t_ring, *key)
                if kind == "st":
                    s, j = rest
                    if j == 0:
                        ck.wait(t_pv, *((b, s - 2) if s >= 2 else (b - 1, s + 6)))
                    act.activation(Pb[4 * (s % 2) + j][:, :], bank[:, :], ACT.Exp).then_inc(t_use.sem, 1)
                    if row:
                        max_row(ck, *row)
                        row = None
                elif kind == "m":
                    g, = rest
                    if g == 1:
                        ck.wait(t_m[0], b)
                    else:
                        ck.wait(t_m[1], b - 1)
                    act.mul(mrow[:, :], bank[0:16, 0:P], -1.0).then_inc(t_use.sem, 1)
                    row = b, g
                else:
                    a, = rest
                    src = bank[:, 0:2 * P].rearrange("p (l j g d) -> p l g j d", l=2, g=2, d=DH)
                    for g in range(2):
                        m = act.copy(VT[i][:, 2 * a:2 * a + 2, g, :, DH * g:DH * g + DH], src[:, :, g, :, :])
                    m.then_inc(t_use.sem, 1)
            if row:
                max_row(ck, *row)

        over_windows(act, body, tail)

    def vector(dve, tail):
        dve.memset(KS[0][:, :, :, :], 0.0).then_inc(t_set[0].sem, 1)

        def small(ck, b, what):
            i = b % 2
            if what == "stats":
                ck.wait(t_x[b % 2], b)
                dve.bn_stats(stats[:, :], xt[i]).then_inc(t_dve.sem, 1)
            elif what == "aggr":
                ck.wait(t_dve, b, "stats", apart=True)
                dve.bn_aggr(mv[i][:, :], stats[:, :]).then_inc(t_dve.sem, 1)
            else:
                ck.wait(t_dc, b)
                ck.wait(t_rs, b - 1)
                dve.reciprocal(rc[:, :], dc[:, :]).then_inc(t_dve.sem, 1)

        def body(ck, w):
            todo = dve_small(w)
            if w < 0:
                small(ck, *todo.pop(0))
                small(ck, *todo.pop(0))
                dve.memset(QS[0][:, :, :, :], 0.0).then_inc(t_set[0].sem, 1)
            if 0 <= w < B:
                for k in range(16):
                    ck.wait(t_nat, w, k)
                    dve.tensor_reduce(mx[:, 2 * k:2 * k + 2], nat[k % 2][:, :, :], AX.X, ALU.max).then_inc(t_max.sem, 1)
                    if todo and (k in (1, 2) and todo[0][1] != "recip" or k == 9):
                        small(ck, *todo.pop(0))
            for job in todo:
                small(ck, *job)
            if w < 0:
                dve.memset(KS[1][:, :, :, :], 0.0).then_inc(t_set[1].sem, 1)
                dve.memset(QS[1][:, :, :, :], 0.0).then_inc(t_set[1].sem, 1)

        over_windows(dve, body, tail)

    def gpsimd(pool, tail):
        for i in range(2):
            pool.memset(VT[i][:, :, :, :, :], 1.0).then_inc(t_vt.sem, 1)
        pool.wait_ge(t_cst.sem, 16)
        def job(ck, b, what):
            i = b % 2
            done = lambda ins: ins.then_inc(t_pool.sem, 1)
            v, m = ln[i], mv[i]
            if what == "na":
                ck.wait(t_ev, b, 1)
                ck.wait(t_pool, b - 1, "att")
                done(pool.tensor_scalar(tn[:, :], U[0][:, :], cme[:, 0:1], 1.0, ALU.mult, ALU.mult))
            elif what == "nb":
                ck.wait(t_st, b - 2)
                done(pool.tensor_scalar(ao[i][:, :], U[1][:, :], cme[:, 1:2], 1.0, ALU.mult, ALU.mult))
            elif what == "num":
                ck.wait(t_pool, b, "nb")
                done(pool.tensor_tensor(tn[:, :], tn[:, :], ao[i][:, :], ALU.add))
            elif what == "att":
                ck.wait(t_rb, b)
                ck.wait(t_pool, b, "num")
                done(pool.tensor_tensor(ao[i][:, :], tn[:, :], rd[:, :], ALU.mult))
            elif what == "negm":
                ck.wait(t_dve, b, "aggr")
                done(pool.tensor_scalar(v[:, 0:1], m[:, 0:1], -1.0, None, ALU.mult))
            elif what == "veps":
                done(pool.tensor_scalar(v[:, 1:2], m[:, 1:2], EPS, None, ALU.add))
            elif what == "rstd":
                ck.wait(t_pool, b, "veps")
                done(pool.tensor_tensor(v[:, 2:3], v[:, 1:2], cst[:, K_PH:K_PH + 1], ALU.pow))
            elif what == "rs":
                ck.wait(t_pool, b, "rstd")
                done(pool.tensor_scalar(v[:, 3:4], v[:, 2:3], SCALE, None, ALU.mult))
            elif what == "qf":
                ck.wait(t_pool, b, "rs")
                done(pool.tensor_scalar(qf[:, :], xt[i], v[:, 0:1], v[:, 3:4], ALU.add, ALU.mult))
            elif what == "qh":
                ck.wait(t_pool, b, "qf")
                ck.wait(t_sq, b - 2)
                done(pool.tensor_scalar(qhl[i][:, 0, :], qf[:, :], 1.0, 1.0, ALU.mult, ALU.mult))
            elif what == "ql":
                ck.wait(t_pool, b, "qh")
                done(pool.tensor_tensor(qhl[i][:, 1, :], qf[:, :], qhl[i][:, 0, :], ALU.subtract))
            elif what == "kh":
                ck.wait(t_c[b % 2], b)
                ck.wait(t_sk, b - 2)
                done(pool.tensor_scalar(khl[i][:, 0, :], ct[i], 1.0, 1.0, ALU.mult, ALU.mult))
            elif what == "kl":
                ck.wait(t_pool, b, "kh")
                done(pool.tensor_tensor(khl[i][:, 1, :], ct[i], khl[i][:, 0, :], ALU.subtract))
            elif what == "wlo":
                ck.wait(t_wh, b)
                cols = bass.ds(ck.index(b) * WCH, WCH)
                done(pool.tensor_tensor(wlo[:, cols], wst[i], whi[:, cols], ALU.subtract))

        def body(ck, w):
            for k in pool_jobs(w):
                tail.get(k, lambda: None)()
                job(ck, *k)
            if w < 0:
                pool.wait_ge(t_gate.sem, 1)
                pool.tensor_tensor(gate[:, 5:6], gate[:, 3:4], gate[:, 2:3], ALU.mult).then_inc(t_gate.sem, 1)
                pool.wait_ge(t_gate.sem, 2)
                pool.tensor_scalar(cme[:, 0:2], cst[:, K_ME:K_ME + 2], gate[:, 5:6], None, ALU.mult).then_inc(t_gate.sem, 1)
                pool.wait_ge(t_gate.sem, 3)

        over_windows(pool, body, tail, apart=True)

    def free_stacks(eng):
        eng.wait_ge(t_ring.sem, t_ring.at[B - 2, "st", 7, 3])

    def free_early(eng):
        eng.wait_ge(t_ring.sem, t_ring.at[B - 2, "st", 7, 3])
        eng.wait_ge(t_pv.sem, t_pv.at[B - 2, 7])
        eng.wait_ge(t_sq.sem, t_sq.value)
        eng.wait_ge(t_sk.sem, t_sk.value)

    def free_products(eng):
        eng.wait_ge(t_pv.sem, t_pv.value)
        eng.wait_ge(t_use.sem, t_use.value)
        eng.wait_ge(t_ev.sem, t_ev.value)

    def free_hosts(eng):
        eng.wait_ge(t_pool.sem, t_pool.at[B - 2, "wlo"])
        eng.wait_ge(t_ring.sem, t_ring.at[B - 1, "vt", 1])

    def free_all(eng):
        eng.wait_ge(t_st.sem, t_st.value)

    def stored(eng, b):
        eng.wait_ge(t_st.sem, t_st.at[b,])

    def scores_read(eng):
        eng.wait_ge(t_max.sem, t_max.value)

    return ({"sync": sync, "tensor": tensor, "scalar": scalar, "vector": vector, "gpsimd": gpsimd},
            {"stacks": free_stacks, "early": free_early, "products": free_products, "hosts": free_hosts, "all": free_all,
             "stored": stored, "scores": scores_read})


ORDER = [3, 7, E, 2, 6, 1, 5, 0, 4]
SEQ = [(e, n) for e in ORDER for n in range(TILES[e])]
G4 = 4
NG = B // G4


def ffn(nc, c, keep, sb, ps, sem, ends, x, att, bcol, b2, rw, rb, upb, coreb, out):
    cst, whi, wlo, gate = keep["cst"], keep["whi"], keep["wlo"], keep["gate"]
    ident = cst[:, K_ID:K_ID + P]
    A = lambda n, s, d=F32: sb(n, s, d, c)
    X, XA, u = keep["X"], keep["XA"], keep["u"]
    uh, ul = A("uh", [P, LB, L], F16), A("ul", [P, LB, L], F16)
    bc, b2s, rws = A("bc", [P, NTS + 2]), A("b2s", [P, LAT]), A("rws", [P, LB, 32])
    rbb, tb, lp = A("rbb", [P, G4, E]), A("tb", [P, L]), A("lp", [P, L])
    gb, zs, Z = A("gb", [P, NT]), A("zs", [P, LAT]), A("Z", [P, LAT])
    st, mv, lnv = A("st4", [P, G4, 6]), A("mv4", [P, G4, 2]), A("ln4", [P, 2, G4])
    uf = A("uf", [P, LB, L])
    gbs = XA[:, :, :].rearrange("p t q -> p (t q)").bitcast(F16)
    gbh, gbl = (gbs[:, k * NT * 32:(k + 1) * NT * 32].rearrange("p (n c) -> p n c", c=32) for k in range(2))
    gf_, gh, gl = A("gf", [P, 2, L]), A("gh", [P, 2, L], F16), A("gl", [P, 2, L], F16)
    lg, pe_, pp, t8, t8i = A("lg", [P, G4, E]), A("pexp", [P, G4, E]), A("pp", [P, G4, E]), A("top", [P, G4, 8]), A("topi", [P, G4, 8], U32)
    red = A("red", [P, 8, G4])
    tif, m1, m2 = A("tif", [P, G4, 2]), A("m1", [P, G4, E]), A("m2", [P, G4, E])
    Gp, GT = A("Gp", [P, G4, P]), A("GT", [P, L])
    af = [A(f"af{i}", [P, L]) for i in range(3)]
    ah = [A(f"ah{i}", [P, L], F16) for i in range(3)]
    al = [A(f"al{i}", [P, L], F16) for i in range(3)]
    acc = A("acc", [P, G4, LAT])
    guh, gul = A("guh", [P, LB, L], F16), A("gul", [P, LB, L], F16)
    XB = A("XB", [P, G4, L])
    oh, ol = A("oh", [P, 2, L], F16), A("ol", [P, 2, L], F16)
    Y = [ps(f"Y{i}", [P, G4, LAT], c) for i in range(2)]
    H = [ps(f"H{i}", [P, L], c) for i in range(4)]

    T = lambda n, step=1: Tally(sem(n), step)
    t_in, t_xx, t_o = T("f_in", 16), T("f_x", 16), T("f_out", 16)
    t_in.plan("all", n=6)
    t_pe, t_act, t_dve, t_pool = T("f_pe"), T("f_act"), T("f_dve"), T("f_pool")

    NA = len(SEQ)
    LAG = 2
    PE_FRONT = {29: ("lg", 0), 30: ("lt", 0), 31: ("h", 0), 33: ("h", 1)}
    pe_ops = []
    for n in range(NA + LAG):
        if n < NA:
            pe_ops.append(("a", n))
        if n == 3:
            pe_ops.append(("gt", 0))
        if n >= LAG:
            pe_ops.append(("y", n - LAG))
        if 24 <= n < 24 + LB:
            pe_ops.append(("uT", n - 24))
        if n in PE_FRONT:
            pe_ops.append(PE_FRONT[n])
    pe_ops += [("core", 0), ("ot", 0), ("ot", 1), ("core", 1), ("fin", 0), ("fin", 1), ("core", 2), ("fin", 2), ("core", 3), ("fin", 3)]
    ring = [("fin", k[1]) if k[0] == "core" else k for k in pe_ops if k[0] not in ("y", "fin")]
    bank = {k: n % 4 for n, k in enumerate(ring)}
    bank["fin", G4 - 1] = 1
    ACT_EMPTIES = ("uT", "lg", "h", "a", "gt")

    def y_last(e):
        return SEQ.index((e, TILES[e] - 1))

    act_ops = []
    for n in range(NA):
        act_ops.append(("a", n))
        if n in (4, 6, 8, 10):
            act_ops.append(("gu", (n - 4) // 2))
        if n == 3:
            act_ops.append(("gt", 0))
        if 24 <= n < 24 + LB:
            act_ops.append(("uT", n - 24))
        if n in PE_FRONT and PE_FRONT[n][0] != "lt":
            act_ops.append(PE_FRONT[n])
    act_ops += [("ot", 0), ("ot", 1)]

    router = ["lred", "lb", "lmx", "lsub", "psum", "prcp", "pp"] + [f"max{t}" for t in range(G4)] + \
             [f"idx{t}" for t in range(G4)] + ["tif", "dz", "e1", "g1", "g2", "m1", "m2", "G1", "G2"]
    steps = {31: router[:4], 36: router[4:11], 37: router[11:17], 38: router[17:]}
    dve_ops = [("r", "G")]
    for n in range(NA):
        dve_ops.append(("al", n))
        if n in (5, 7, 9, 11):
            dve_ops.append(("gul", (n - 5) // 2))
        if n >= 3 and SEQ[n - 3][1] == TILES[SEQ[n - 3][0]] - 1:
            dve_ops += [("acc", SEQ[n - 3][0], t) for t in range(G4)]
        if 14 <= n < 14 + G4:
            dve_ops.append(("stats", n - 14))
        if n == 18:
            dve_ops += [("aggr", t) for t in range(G4)]
        if 25 <= n < 25 + LB:
            dve_ops.append(("ul", n - 25))
        dve_ops += [("r", what) for what in steps.get(n, ())]
    dve_ops += [("gl", 0), ("gl", 1)]
    done = {o[1] for o in dve_ops if o[0] == "acc"}
    dve_ops += [("acc", e, t) for e in ORDER if e not in done for t in range(G4)]
    dve_ops += [("ot", 0), ("ot", 1)] + [("fin", t) for t in range(G4)]

    pool_ops = []
    for n in range(NA):
        pool_ops.append(("ah", n))
        if n in (5, 7, 9, 11):
            pool_ops.append(("guh", (n - 5) // 2))
        if n in (2, 3, 4, 6):
            pool_ops.append(("xb", (2, 3, 4, 6).index(n)))
        if 14 <= n < 14 + G4:
            pool_ops.append(("x1", n - 14))
        if n == 19:
            pool_ops += [("negm", 0), ("rstd", 0), ("rstd", 1)]
        if 20 <= n < 20 + G4:
            pool_ops.append(("u", n - 20))
        if 25 <= n < 25 + LB:
            pool_ops.append(("uh", n - 25))
        if 32 <= n < 32 + G4:
            pool_ops.append(("pexp", n - 32))
        if n == 38:
            pool_ops.append(("e2", 0))
    pool_ops += [("gh", 0), ("gh", 1)]
    FRONT = ("x1", "stats", "aggr", "negm", "rstd", "u", "uT", "uh", "ul", "lg", "lt", "h", "gh", "gl", "r", "pexp", "e2")

    def ahead(op):
        return int(op[0] in FRONT and op != ("r", "G"))

    def of_group(ops, r):
        if r < 0:
            late = {("pexp", 0): 1, ("gh", 0): 2, ("pexp", 1): 3, ("gh", 1): 4, ("pexp", 2): 5, ("pexp", 3): 5, ("e2", 0): 6}
            ops = sorted(ops, key=lambda op: 6 if op[0] == "r" and op[1] not in router[:4] else late.get(op, 0))
        for op in ops:
            if 0 <= r + ahead(op) < NG:
                yield (r + ahead(op), *op)

    for r in range(-1, NG):
        for tally, ops in ((t_pe, pe_ops), (t_act, act_ops), (t_dve, dve_ops), (t_pool, pool_ops)):
            for k in of_group(ops, r):
                tally.plan(*k)
        if r + 1 < NG:
            t_xx.plan(r + 1, n=2)
        if r >= 0:
            t_o.plan(r, n=G4)
    t_z, t_zd, t_zp = T("f_z"), T("f_zd"), T("f_zp")

    def first_front(eng, ops, do, *names):
        for k in of_group(ops, -1):
            if k[1] in (names or LATE):
                do(Clock(eng, 1, t_in), *k)

    LATE = set(FRONT) - {"x1", "stats", "aggr", "negm", "rstd", "u", "uT", "e2"}

    def over_groups(eng, ops, do, apart=False):
        ck = Clock(eng, 1, t_in, apart)
        ended = False
        for k in of_group(ops, 0):
            if k[1] in ("guh", "gul", "xb", "ot") and not ended:
                ends["all"](eng)
                ended = True
            do(ck, *k)
        with eng.Fori(0, NG - 2) as turn:
            ck.turn = turn
            for k in of_group(ops, 1):
                do(ck, *k)
        ck.turn = None
        for k in of_group(ops, NG - 1):
            do(ck, *k)

    def sync(sp):
        def loads(ck, r):
            for t in range(G4):
                ck.wait(t_pool, r - 1, "xb", t)
            ck.wait(t_dve, r - 1, "stats", G4 - 1)
            ck.wait(t_pool, r - 1, "u", G4 - 1)
            rows = bass.ds(ck.index(r) * G4, G4)
            sp.dma_start(X[:, :, :], x[rows].rearrange("t p q -> p t q")).then_inc(t_xx.sem, 16)
            sp.dma_start(XA[:, :, :], att[rows].rearrange("t p q -> p t q")).then_inc(t_xx.sem, 16)

        def body(ck, r):
            if r + 1 < NG:
                loads(ck, r + 1)
            for t in range(G4):
                ck.wait(t_dve, r, "fin", t)
                sp.dma_start(out[ck.index(r) * G4 + t], XB[:, t, :]).then_inc(t_o.sem, 16)

        ck = Clock(sp, 1, t_in, apart=True)

        def in_15():
            ends["hosts"](sp)
            ends["stored"](sp, G4 - 1)
            loads(ck, 0)

        def before_16():
            ends["stacks"](sp)
            for dst, src in ((bc[:, :], bcol), (b2s[:, :], b2), (rws[:, :, :], rw), (tb[:, :], upb.partition_broadcast(P)),
                             (lp[:, :], coreb.partition_broadcast(P)),
                             (rbb[:, :, :], rb.unsqueeze(0).broadcast_to([G4, E]).partition_broadcast(P))):
                sp.dma_start(dst, src).then_inc(t_in.sem, 16)

        def rest():
            sp.wait_ge(t_z.sem, 4)
            ends["all"](sp)
            body(ck, 0)
            with sp.Fori(0, NG - 2) as turn:
                ck.turn = turn
                body(ck, 1)
            ck.turn = None
            body(ck, NG - 1)
            sp.wait_ge(t_o.sem, t_o.value)

        return {(B - 1, "loads"): in_15, B: before_16}, rest

    def tensor(pe):
        def three(dst, wc, mh, ml, first, last, swap=False, skip=False):
            for n, (a, b) in enumerate(((whi, mh), (wlo, mh), (whi, ml))):
                l, r = (b, a[:, wc]) if swap else (a[:, wc], b)
                m = pe.matmul(dst, l, r, start=first and n == 0, stop=last and n == 2, skip_group_check=skip)
            return m

        def bias_products(lo, hi):
            for n in range(lo, hi, 4):
                for k, (g_, w_, q) in enumerate((g_, w_, q) for g_, w_ in ((gbh, whi), (gbl, whi), (gbh, wlo)) for q in range(4)):
                    wc = slice(C_W2 + (n + q) * LAT, C_W2 + (n + q + 1) * LAT)
                    m = pe.matmul(Y[0][32 * q:32 * q + 32, 0, :], g_[:, n + q, :], w_[:, wc],
                                  start=(n == 0 and k < 4), stop=(n == NT - 4 and k >= 8))
            return m

        def last_user(ck, r, key):
            same = [k for k in ring if bank[k] == bank[key]]
            p, turn = same.index(key), r - ahead(key)
            before = [(turn + ahead(k), k) for k in reversed(same[:p])] + [(turn - 1 + ahead(k), k) for k in reversed(same)]
            for group, k in before:
                if 0 <= group < NG:
                    reader = t_act if k[0] in ACT_EMPTIES else t_dve
                    return ck.wait(reader, group, *(("r", "lred") if k[0] == "lt" else k))

        def do(ck, r, name, i):
            key = (name, i) if name != "core" else ("fin", i)
            if key in bank and not (name == "fin"):
                last_user(ck, r, key)
            if name != "y":
                dst = H[bank[key]]
            if name == "uT":
                if i == 0:
                    for t in range(G4):
                        ck.wait(t_pool, r, "u", t)
                for t in range(G4):
                    m = pe.transpose(dst[:, t * P:t * P + P], u[:, t, i * P:i * P + P], ident)
            elif name == "lg":
                for k in range(LB):
                    ck.wait(t_act, r, "uT", k)
                    m = pe.matmul(dst[32 * k:32 * k + 32, :], rws[:, k, :], uf[:, k, :], start=True, stop=True)
            elif name == "lt":
                ck.wait(t_act, r, "lg", 0)
                for t in range(G4):
                    m = pe.transpose(dst[:, t * P:t * P + P], lp[:, t * P:t * P + P], ident)
            elif name == "h":
                for k in range(LB):
                    if i == 0:
                        ck.wait(t_pool, r, "uh", k)
                        ck.wait(t_dve, r, "ul", k)
                    c0 = C_DOWN + k * LAT + i * P
                    m = three(dst[:, :], slice(c0, c0 + P), uh[:, k, :], ul[:, k, :], k == 0, k == LB - 1)
            elif name == "a":
                if i == 0:
                    for k in range(2):
                        ck.wait(t_pool, r, "gh", k)
                        ck.wait(t_dve, r, "gl", k)
                e, n = SEQ[i]
                for k in range(2):
                    c0 = C_W1 + (FIRST[e] + n) * LAT + k * P
                    m = three(dst[:, :], slice(c0, c0 + P), gh[:, k, :], gl[:, k, :], k == 0, k == 1)
            elif name == "gt":
                ck.wait(t_dve, r, "r", "G")
                for t in range(G4):
                    m = pe.transpose(dst[:, t * P:t * P + P], Gp[:, t, :], ident)
            elif name == "y":
                e, n = SEQ[i]
                o = ORDER.index(e)
                if i == 0 and r == 0:
                    pe.wait_ge(t_z.sem, 7)
                if n == 0:
                    if o >= 2:
                        ck.wait(t_dve, r, "acc", ORDER[o - 2], G4 - 1)
                    else:
                        ck.wait(t_dve, r - 1, "acc", ORDER[-1], G4 - 1)
                ck.wait(t_pool, r, "ah", i)
                ck.wait(t_dve, r, "al", i)
                for t in range(G4):
                    first = n == 0 and t % 2 == 0
                    dst = Y[o % 2][:, t, :]
                    if e == E and n == 0:
                        if t == 0:
                            ck.wait(t_act, r, "gt", 0)
                        pe.matmul(dst, GT[:, t * P:t * P + P], Z[:, :], start=first, stop=False, skip_group_check=True)
                        first = False
                    c0 = C_W2 + (FIRST[e] + n) * LAT
                    cols = slice(t * P, t * P + P)
                    m = three(dst, slice(c0, c0 + LAT), ah[i % 3][:, cols], al[i % 3][:, cols], first,
                              n == TILES[e] - 1, swap=True, skip=True)
            elif name == "core":
                for k in range(LB):
                    if i == 0:
                        ck.wait(t_pool, r, "guh", k)
                        ck.wait(t_dve, r, "gul", k)
                    c0, cols = C_CORE + k * L, slice(i * P, i * P + P)
                    m = three(dst[:, :], slice(c0, c0 + L), guh[:, k, cols], gul[:, k, cols], k == 0, False, swap=True)
            elif name == "ot":
                for t in range(G4):
                    if i == 0:
                        ck.wait(t_dve, r, "acc", ORDER[-1], t)
                    m = pe.transpose(dst[:, t * P:t * P + P], acc[:, t, i * P:i * P + P], ident)
            elif name == "fin":
                for k in range(2):
                    if i == 0:
                        ck.wait(t_dve, r, "ot", k)
                    c0, cols = C_UP + k * L, slice(i * P, i * P + P)
                    m = three(dst[:, :], slice(c0, c0 + L), oh[:, k, cols], ol[:, k, cols], False, k == 1, swap=True)
            m.then_inc(t_pe.sem, 1)

        def rest():
            ends["scores"](pe)
            ends["products"](pe)
            first_front(pe, pe_ops, do, "uT")
            pe.wait_ge(t_z.sem, 3)
            bias_products(0, 12)
            first_front(pe, pe_ops, do, "lg")
            bias_products(12, 24)
            first_front(pe, pe_ops, do, "lt", "h")
            bias_products(24, NT).then_inc(t_z.sem, 1)
            pe.wait_ge(t_z.sem, 5)
            pe.matmul(Y[1][:, 0, :], cst[:, K_M1:K_M1 + P], zs[:, :], start=True, stop=False)
            pe.matmul(Y[1][:, 0, :], cst[:, K_M2:K_M2 + P], b2s[:, :], start=False, stop=True).then_inc(t_z.sem, 1)
            over_groups(pe, pe_ops, do)

        return {}, rest

    def scalar(act):
        def do(ck, r, name, i):
            if name in ("uT", "lg", "h", "a", "gt", "ot"):
                src = H[bank[(name, i)]][:, :]
                ck.wait(t_pe, r, name, i)
            if name == "uT":
                ck.wait(t_pool, r - 1, "guh", i)
                ck.wait(t_dve, r - 1, "gul", i)
                m = act.copy(uf[:, i, :], src)
            elif name == "lg":
                m = act.copy(lp[:, :], src)
            elif name == "h":
                m = act.activation(gf_[:, i, :], src, ACT.Gelu, bias=bc[:, NTS + i:NTS + i + 1])
            elif name == "a":
                e, n = SEQ[i]
                ck.wait(t_pool, *((r, "ah", i - 3) if i >= 3 else (r - 1, "ah", i - 3 + NA)))
                ck.wait(t_dve, *((r, "al", i - 3) if i >= 3 else (r - 1, "al", i - 3 + NA)))
                b_ = FIRST[e] + n
                m = act.activation(af[i % 3][:, :], src, ACT.Gelu, bias=bc[:, b_:b_ + 1])
            elif name == "gu":
                ck.wait(t_pool, r, "uh", i)
                ck.wait(t_dve, r, "ul", i)
                ck.wait(t_pe, r, "lg", 0)
                m = act.activation(uf[:, i, :], uf[:, i, :], ACT.Gelu)
            elif name == "gt":
                m = act.copy(GT[:, :], src)
            elif name == "ot":
                ck.wait(t_pe, r - 1, "fin", G4 - 1)
                m = act.copy(oh[:, i, :], src)
            m.then_inc(t_act.sem, 1)

        def before_17():
            ends["early"](act)
            act.wait_ge(t_in.sem, t_in.value)
            act.activation(gb[:, :], bc[:, 0:NT], ACT.Gelu).then_inc(t_z.sem, 1)

        def rest():
            first_front(act, act_ops, do, "uT")
            act.wait_ge(t_zp.sem, 1)
            ends["products"](act)
            first_front(act, act_ops, do)
            act.wait_ge(t_z.sem, 4)
            act.copy(zs[:, :], Y[0][:, 0, :]).then_inc(t_z.sem, 1)
            act.wait_ge(t_z.sem, 6)
            act.copy(Z[:, :], Y[1][:, 0, :]).then_inc(t_z.sem, 1)
            over_groups(act, act_ops, do)

        return {B + 1: before_17}, rest

    def vector(dve):
        wide = lambda v: v.unsqueeze(2).broadcast_to([P, G4, E])
        R = lambda n: red[:, n, :]
        iota = cst[:, K_IOTA:K_IOTA + E].unsqueeze(1).broadcast_to([P, G4, E])

        def route(ck, r, what):
            own = lambda n, apart=False: ck.wait(t_dve, r, "r", n, apart=apart)
            if what == "lred":
                ck.wait(t_pe, r, "lt", 0)
                src = H[bank[("lt", 0)]][:, :].rearrange("p (t k c) -> p t c k", t=G4, k=LB)
                return dve.tensor_reduce(lg[:, :, :], src[:, :, 0:E, :], AX.X, ALU.add)
            if what == "lb":
                own("lred")
                return dve.tensor_tensor(lg[:, :, :], lg[:, :, :], rbb[:, :, :], ALU.add)
            if what == "lmx":
                own("lb")
                return dve.tensor_reduce(R(0), lg[:, :, :], AX.X, ALU.max)
            if what == "lsub":
                own("lmx")
                return dve.tensor_tensor(lg[:, :, :], lg[:, :, :], wide(R(0)), ALU.subtract)
            if what == "psum":
                ck.wait(t_pool, r, "pexp", G4 - 1)
                return dve.tensor_reduce(R(1), pe_[:, :, :], AX.X, ALU.add)
            if what == "prcp":
                own("psum")
                return dve.reciprocal(R(2), R(1))
            if what == "pp":
                own("prcp")
                return dve.tensor_tensor(pp[:, :, :], pe_[:, :, :], wide(R(2)), ALU.mult)
            if what[:3] == "max":
                own("pp", apart=True)
                t = int(what[3:])
                return dve.max(t8[:, t, :], pp[:, t, :])
            if what[:3] == "idx":
                own("max" + what[3:], apart=True)
                t = int(what[3:])
                return dve.max_index(t8i[:, t, :], t8[:, t, :], pp[:, t, :])
            if what == "tif":
                own("idx3")
                return dve.tensor_copy(tif[:, :, :], t8i[:, :, 0:2])
            if what == "dz":
                return dve.tensor_tensor(R(3), t8[:, :, 1], t8[:, :, 0], ALU.subtract)
            if what == "e1":
                ck.wait(t_pool, r, "e2", 0)
                return dve.tensor_scalar(R(5), R(4), 1.0, None, ALU.add)
            if what == "g1":
                own("e1")
                return dve.reciprocal(R(6), R(5))
            if what == "g2":
                own("g1")
                return dve.tensor_tensor(R(7), R(4), R(6), ALU.mult)
            if what in ("m1", "m2"):
                own("tif")
                n = int(what[1]) - 1
                return dve.tensor_tensor((m1, m2)[n][:, :, :], iota, wide(tif[:, :, n]), ALU.is_equal)
            if what in ("G1", "G2"):
                n = int(what[1]) - 1
                own("m1" if n == 0 else "m2")
                own("g2")
                m = (m1, m2)[n][:, :, :]
                return dve.tensor_tensor(m, m, wide(R(6 + n)), ALU.mult)
            own("G2")
            ck.wait(t_pe, r - 1, "gt", 0)
            ck.wait(t_dve, r - 1, "acc", ORDER[-1], G4 - 1)
            return dve.tensor_tensor(Gp[:, :, 0:E], m1[:, :, :], m2[:, :, :], ALU.add)

        def do(ck, r, name, i, t=None):
            if name == "ul":
                ck.wait(t_act, r, "uT", i)
                ck.wait(t_pool, r, "uh", i)
                ck.wait(t_pe, r - 1, "h", 1)
                m = dve.tensor_tensor(ul[:, i, :], uf[:, i, :], uh[:, i, :], ALU.subtract)
            elif name == "gl":
                ck.wait(t_pool, r, "gh", i)
                m = dve.tensor_tensor(gl[:, i, :], gf_[:, i, :], gh[:, i, :], ALU.subtract)
            elif name == "gul":
                ck.wait(t_pool, r, "guh", i)
                m = dve.tensor_tensor(gul[:, i, :], uf[:, i, :], guh[:, i, :], ALU.subtract)
            elif name == "al":
                ck.wait(t_pool, r, "ah", i)
                if SEQ[i][0] == E:
                    m = dve.scalar_tensor_tensor(out=al[i % 3][:, :], in0=af[i % 3][:, :], scalar=0.1, in1=ah[i % 3][:, :],
                                                 op0=ALU.mult, op1=ALU.subtract)
                else:
                    m = dve.tensor_tensor(al[i % 3][:, :], af[i % 3][:, :], ah[i % 3][:, :], ALU.subtract)
            elif name == "acc":
                e = i
                o = ORDER.index(e)
                if t == 0:
                    ck.wait(t_pe, r, "y", y_last(e))
                y = Y[o % 2][:, t, :]
                a = acc[:, t, :]
                if o == 0:
                    ck.wait(t_pe, r - 1, "ot", 1)
                    ck.wait(t_dve, r, "r", "G")
                    m = dve.tensor_scalar(a, y, Gp[:, t, e:e + 1], None, ALU.mult)
                else:
                    ck.wait(t_dve, r, "acc", ORDER[o - 1], t)
                    if e == E:
                        m = dve.tensor_tensor(a, y, a, ALU.add)
                    else:
                        m = dve.scalar_tensor_tensor(out=a, in0=y, scalar=Gp[:, t, e:e + 1], in1=a, op0=ALU.mult, op1=ALU.add)
            elif name == "stats":
                ck.wait(t_pool, r, "x1", i)
                m = dve.bn_stats(st[:, i, :], X[:, i, :])
            elif name == "aggr":
                ck.wait(t_dve, r, "stats", i, apart=True)
                m = dve.bn_aggr(mv[:, i, :], st[:, i, :])
            elif name == "ot":
                ck.wait(t_act, r, "ot", i)
                m = dve.tensor_tensor(ol[:, i, :], H[bank[("ot", i)]][:, :], oh[:, i, :], ALU.subtract)
            elif name == "fin":
                ck.wait(t_pe, r, "fin", i)
                ck.wait(t_pool, r, "xb", i)
                m = dve.scalar_tensor_tensor(out=XB[:, i, :], in0=H[bank[("fin", i)]][:, :], scalar=gate[:, 4:5],
                                             in1=XB[:, i, :], op0=ALU.mult, op1=ALU.add)
            elif name == "r":
                m = route(ck, r, i)
            m.then_inc(t_dve.sem, 1)

        def before_16():
            ends["stacks"](dve)
            first_front(dve, dve_ops, do, "stats", "aggr")
            dve.memset(gbh[:, :, :], 0.0).then_inc(t_zd.sem, 1)
            dve.memset(gbl[:, :, :], 0.0).then_inc(t_zd.sem, 1)
            dve.wait_ge(t_in.sem, t_in.value)
            dve.tensor_tensor(rbb[:, :, :], rbb[:, :, :], cst[:, K_COST:K_COST + G4 * E].rearrange("p (t e) -> p t e", t=G4),
                              ALU.subtract).then_inc(t_zd.sem, 1)

        def before_17():
            dve.wait_ge(t_zd.sem, 3)
            dve.wait_ge(t_z.sem, 1)
            for e in range(E):
                n = slice(FIRST[e], FIRST[e] + TILES[e])
                m = dve.tensor_copy(gbh[:, n, e], gb[:, n])
            m.then_inc(t_z.sem, 1)
            dve.wait_ge(t_z.sem, 2)
            for e in range(E):
                n = slice(FIRST[e], FIRST[e] + TILES[e])
                m = dve.tensor_tensor(gbl[:, n, e], gb[:, n], gbh[:, n, e], ALU.subtract)
            m.then_inc(t_z.sem, 1)

        def rest():
            ends["products"](dve)
            dve.memset(Gp[:, :, :], 0.0).then_inc(t_zd.sem, 1)
            dve.wait_ge(t_zd.sem, 4)
            dve.memset(Gp[:, :, E:E + 1], 1.0).then_inc(t_zd.sem, 1)
            dve.wait_ge(t_zd.sem, 5)
            first_front(dve, dve_ops, do)
            over_groups(dve, dve_ops, do)

        return {B: before_16, B + 1: before_17}, rest

    def gpsimd(pool):
        cast = lambda dst, src, by=1.0: pool.tensor_scalar(dst, src, by, 1.0, ALU.mult, ALU.mult)
        base = cst[:, K_E:K_E + G4 * E]

        def do(ck, r, name, i):
            if name == "uh":
                ck.wait(t_act, r, "uT", i)
                ck.wait(t_pe, r - 1, "h", 1)
                m = cast(uh[:, i, :], uf[:, i, :])
            elif name == "gh":
                ck.wait(t_act, r, "h", i)
                ck.wait(t_pe, r - 1, "a", NA - 1)
                m = cast(gh[:, i, :], gf_[:, i, :])
            elif name == "guh":
                ck.wait(t_act, r, "gu", i)
                ck.wait(t_pe, r - 1, "fin", G4 - 1)
                m = cast(guh[:, i, :], uf[:, i, :])
            elif name == "ah":
                ck.wait(t_act, r, "a", i)
                ck.wait(t_pe, *((r, "y", i - 3) if i >= 3 else (r - 1, "y", i - 3 + NA)))
                m = cast(ah[i % 3][:, :], af[i % 3][:, :], 0.1 if SEQ[i][0] == E else 1.0)
            elif name == "pexp":
                ck.wait(t_dve, r, "r", "lsub")
                m = pool.tensor_tensor(pe_[:, i, :], base[:, 0:E], lg[:, i, :], ALU.pow)
            elif name == "e2":
                ck.wait(t_dve, r, "r", "dz")
                m = pool.tensor_tensor(red[:, 4, :], base[:, 0:G4], red[:, 3, :], ALU.pow)
            elif name == "xb":
                ck.wait(t_o, r - 1)
                m = pool.tensor_tensor(XB[:, i, :], X[:, i, :], tb[:, :], ALU.add)
            elif name == "x1":
                ck.wait(t_xx, r)
                m = pool.tensor_tensor(X[:, i, :], X[:, i, :], XA[:, i, :], ALU.add)
            elif name == "negm":
                ck.wait(t_dve, r, "aggr", G4 - 1)
                m = pool.tensor_scalar(lnv[:, 0, :], mv[:, :, 0], -1.0, 1.0, ALU.mult, ALU.mult)
            elif name == "rstd" and i == 0:
                m = pool.tensor_scalar(lnv[:, 1, :], mv[:, :, 1], EPS, None, ALU.add)
            elif name == "rstd":
                ck.wait(t_pool, r, "rstd", 0)
                m = pool.tensor_tensor(lnv[:, 1, :], lnv[:, 1, :], cst[:, K_PH:K_PH + 1].broadcast_to([P, G4]), ALU.pow)
            elif name == "u":
                ck.wait(t_pool, r, "rstd", 1)
                ck.wait(t_pe, r - 1, "uT", LB - 1)
                m = pool.tensor_scalar(u[:, i, :], X[:, i, :], lnv[:, 0, i:i + 1], lnv[:, 1, i:i + 1], ALU.add, ALU.mult)
            m.then_inc(t_pool.sem, 1)

        def before_att_14():
            first_front(pool, pool_ops, do, "x1", "negm", "rstd", "u")
            pool.wait_ge(t_in.sem, t_in.value)
            pool.tensor_tensor(tb[:, :], tb[:, :], lp[:, :], ALU.add).then_inc(t_zp.sem, 1)
            pool.wait_ge(t_zp.sem, 1)
            pool.tensor_scalar(tb[:, :], tb[:, :], gate[:, 4:5], 1.0, ALU.mult, ALU.mult).then_inc(t_zp.sem, 1)

        def rest():
            first_front(pool, pool_ops, do, "e2")
            over_groups(pool, pool_ops, do, apart=True)

        def before_att_15():
            pool.wait_ge(t_zp.sem, 2)
            ends["products"](pool)
            first_front(pool, pool_ops, do)

        return {(B - 2, "att"): before_att_14, (B - 1, "att"): before_att_15}, rest

    return {"sync": sync, "tensor": tensor, "scalar": scalar, "vector": vector, "gpsimd": gpsimd}


def kernel(**inputs):
    import concourse.bacc as bacc
    from concourse.bass_utils import run_bass_kernel_spmd

    nc = bacc.Bacc("TRN2", target_bir_lowering=False, num_devices=1)
    wall, bcol, b2, rw = pack(inputs)
    g = lambda n: np.ascontiguousarray(inputs[n])
    data = {
        "x": g("x"), "ctx_kv": g("ctx_2048"), "gx": g("g_xattn"), "gf": g("g_ffn"),
        "gamma": g("L0_xattn_gamma").reshape(1), "wall": wall, "bcol": bcol, "b2": b2, "rw": rw,
        "rb": g("L0_ffn_router_b"), "upb": g("L0_ffn_up_b"), "coreb": g("L0_ffn_core_b"),
        "const": constants(), "ones": np.ones((1, 2 * QUADS * L), np.float16),
    }
    args = {n: nc.dram_tensor(f"in_{n}", a.shape, mybir.dt.from_np(a.dtype), kind="ExternalInput").ap()
            for n, a in data.items()}
    out = nc.dram_tensor("out_0", (B, D, L), F32, kind="ExternalOutput").ap()
    program(nc, *args.values(), out)
    r = run_bass_kernel_spmd(nc, [{f"in_{n}": a for n, a in data.items()}], core_ids=[0])
    return r.results[0]["out_0"]
```
